# Optimizing a Trainium2 kernel written in Bass

```python
import numpy as np
import jax
import jax.numpy as jnp

def _softmax(x, axis=-1):
    return jax.nn.softmax(x, axis=axis)

def _gelu(x):
    return jax.nn.gelu(x, approximate=True)

def _silu(x):
    return jax.nn.silu(x)

def _sigmoid(x):
    return jax.nn.sigmoid(x)

def _layernorm(x, axis=-1, eps=1e-05):
    m = jnp.mean(x, axis=axis, keepdims=True)
    v = jnp.var(x, axis=axis, keepdims=True)
    return (x - m) / jnp.sqrt(v + eps)

def _scatter_add(tgt, idx, src, axis=0):
    return tgt.at[idx].add(src)

def _segment_sum(src, seg, n):
    return jax.ops.segment_sum(src, seg, n)
kernel_name = 'mk_adj_resnorm_d2_adj_r2_18570c'

def setup_inputs(seed: int=0):
    np.random.seed(seed)
    _w = jnp.asarray

    def _rec_inputs():
        import jax
        import jax.numpy as jnp
        _gk = jax.random.key(seed)
        x = -0.0005207 + 1.001 * jax.random.normal(jax.random.fold_in(_gk, 1), (4096, 128), jnp.float32)
        _a = jax.random.bernoulli(jax.random.fold_in(_gk, 2), 0.00390625, (4096, 4096))
        _a = jnp.logical_or(_a, jnp.swapaxes(_a, -1, -2))
        _a = jnp.logical_or(_a, jnp.eye(4096, dtype=bool))
        _af = _a.astype(jnp.float32)
        _af = _af * jax.random.uniform(jax.random.fold_in(_gk, 3), (4096, 4096), jnp.float32, 0.05, 5.41998)
        adj = _af
        return (x, adj)
    x, adj = _rec_inputs()

    def _L0_gnn_setup():
        import jax, jax.numpy as jnp
        import numpy as np
        N = 4096
        C = 128
        key = jax.random.key(seed)
        k1, k2, k3 = jax.random.split(key, 3)
        x = jax.random.normal(k1, (N, C), dtype=jnp.float32)
        evals = jax.random.uniform(k2, (N,), dtype=jnp.float32)
        evecs = jax.random.normal(k3, (N, N), dtype=jnp.float32)
        t = jnp.ones((1,), dtype=jnp.float32)
        return {'x': x, 'evals': evals, 'evecs': evecs, 't': t}
    _L0_gnn_all = _L0_gnn_setup()
    _L0_gnn_in = {k: v for k, v in _L0_gnn_all.items() if k in ('evals', 't')}
    del _L0_gnn_all

    def _L1_gnn_setup():
        import jax, jax.numpy as jnp
        import numpy as np
        key = jax.random.key(seed)
        k1, k2, k3, k4 = jax.random.split(key, 4)
        N, H = (4096, 128)
        inputs = jax.random.normal(k1, (N, H), dtype=jnp.float32)
        adj = jax.random.uniform(k2, (N, N), dtype=jnp.float32)
        W = jax.random.normal(k3, (H, H), dtype=jnp.float32)
        b = jax.random.normal(k4, (H,), dtype=jnpp.float32) if False else jax.random.normal(k4, (H,), dtype=jnp.float32)
        return {'inputs': inputs, 'adj': adj, 'W': W, 'b': b}
    _L1_gnn_all = _L1_gnn_setup()
    _L1_gnn_in = {k: v for k, v in _L1_gnn_all.items() if k in ('W', 'b')}
    del _L1_gnn_all
    return {'x': x, 'adj': adj, 'L0_gnn_evals': _L0_gnn_in['evals'], 'L0_gnn_t': _L0_gnn_in['t'], 'L1_gnn_W': _L1_gnn_in['W'], 'L1_gnn_b': _L1_gnn_in['b']}

def reference(x, adj, L0_gnn_evals, L0_gnn_t, L1_gnn_W, L1_gnn_b):
    import jax
    import jax.numpy as jnp

    def _L0_gnn_ref(x, evals, evecs, t):
        import jax, jax.numpy as jnp
        import numpy as np
        N = 4096
        C = 128
        t_eff = jnp.clip(t[0], 1e-08, None)
        x_spec = jnp.einsum('nk,nc->kc', evecs, x)
        coefs = jnp.exp(-evals * t_eff)[:, None]
        out = jnp.einsum('nk,kc->nc', evecs, coefs * x_spec)
        return out

    def _L1_gnn_ref(inputs, adj, W, b):
        import jax, jax.numpy as jnp
        import numpy as np
        N = adj.shape[0]
        adj_hat = adj + jnp.eye(N, dtype=adj.dtype)
        deg = jnp.sum(adj_hat, axis=1, keepdims=True)
        adj_norm = adj_hat / deg
        pre_sup = inputs @ W
        out = adj_norm @ pre_sup + b
        return jnp.tanh(out)
    x = _layernorm(x + _L0_gnn_ref(x, L0_gnn_evals, adj, L0_gnn_t), axis=-1)
    x = _layernorm(x + _L1_gnn_ref(x, adj, L1_gnn_W, L1_gnn_b), axis=-1)
    return x

_drawn_inputs = setup_inputs


def setup_inputs(seed=0):
    import zlib

    import numpy as np

    out = dict(_drawn_inputs(seed))
    spreads = {}
    factors = {}
    for name, (base, spread) in spreads.items():
        noise = np.random.default_rng([zlib.crc32(name.encode()), seed]).standard_normal(out[name].shape)
        drawn = base * np.exp(spread * noise) if base else spread * noise
        out[name] = jnp.asarray(drawn.astype(out[name].dtype))
    for name, factor in factors.items():
        out[name] = (out[name] * factor).astype(out[name].dtype)
    return out
```

```python
import concourse.bass as bass
from concourse import mybir
from contextlib import ExitStack


def spectral_then_graph_conv(nc, x, adj, evals, t, W, b, out):
    f32 = mybir.dt.float32
    f32r = mybir.dt.float32r
    ALU = mybir.AluOpType
    ACT = mybir.ActivationFunctionType

    P = 128
    N, C = x.shape
    assert C == P and N % (4 * P) == 0
    R = 4
    CW = 512
    NG = N // (R * P)
    NK = N // CW
    JB = CW // P
    PAIRS = 2 * NK
    RING = 4
    LAG = 2
    LAST = NG - 1
    EPS = 1e-5
    assert NG == NK and NG % 2 == 0

    ORDER = {2: list(range(NK)), 3: [*range(1, NK), 0]}

    AT_ACC, AT_TURN, AT_SUM = 2, 4, 5
    AT_X1T, AT_X1T_OUT, AT_P, AT_P_OUT = 10, 11, 12, 13
    AT_TANH, AT_STATS3, AT_STORE = 8, 10, 15

    adj_v = adj.rearrange("(g r p) (k w) -> g k p r w", r=R, p=P, w=CW)
    x_v = x.rearrange("(j p) c -> p j c", p=P)
    out_v = out.rearrange("(g r p) c -> g p r c", r=R, p=P)

    ctx = ExitStack()
    with ctx:
        def sb(name, shape, dt=f32):
            return ctx.enter_context(nc.sbuf_tensor(name, shape, dt))

        def sem(name):
            return ctx.enter_context(nc.semaphore(name))

        raw = sb("raw", [P, NK, R, CW])
        hi = sb("hi", [P, RING, 2 * CW], f32r)
        lo = sb("lo", [P, RING, 2 * CW], f32r)
        x_sb = sb("x_sb", [P, NG, R * C])
        xg_hi = sb("xg_hi", [P, 2, R * C], f32r)
        xg_lo = sb("xg_lo", [P, 2, R * C], f32r)
        s_hi = sb("s_hi", [P, N // P * C], f32r)
        s_lo = sb("s_lo", [P, N // P * C], f32r)
        p_hi = sb("p_hi", [P, NG, R * C], f32r)
        p_lo = sb("p_lo", [P, NG, R * C], f32r)
        stage = sb("stage", [P, 2, CW])
        x1_g = sb("x1_g", [P, R * C])
        h_g = sb("h_g", [P, R * C])
        th_g = sb("th_g", [P, R * C])
        y_g = sb("y_g", [P, R * C])
        o_g = sb("o_g", [P, R * C])
        ident = sb("ident", [P, P])
        w_sb = sb("w_sb", [P, C])
        b_bc = sb("b_bc", [P, C])
        ev = sb("ev", [N // P, P])
        t_bc = sb("t_bc", [N // P, 1])
        neg_t = sb("neg_t", [N // P, 1])
        ex = sb("ex", [N // P, P])
        coef = sb("coef", [P, N // P])
        rsum = sb("rsum", [P, NG, R * NK])
        deg = sb("deg", [P, R])
        deg1 = sb("deg1", [P, R])
        rdeg = sb("rdeg", [P, R])
        stats = sb("stats", [P, R, 6])
        msum, mdif, m2, mean, between, var = (sb(n, [P, R]) for n in ("msum", "mdif", "m2", "mean", "between", "var"))
        cen_g = sb("cen_g", [P, R * C])
        eps_sb = sb("eps_sb", [P, R])
        veps = sb("veps", [P, R])
        rstd = sb("rstd", [P, R])
        mhalf = sb("mhalf", [P, R])

        ps = ctx.enter_context(nc.psum_tensor("ps", [P, 8, CW], f32))
        acc = ps[:, 4:6, :]
        bank_a = ps[:, 6, :]
        bank_b = ps[:, 7, :]

        raw_in = [sem(f"raw_in{k}") for k in range(NK)]
        x_in, x_rest_in, w_in, b_in, ev_in, t_in = map(sem, ("x_in", "x_rest_in", "w_in", "b_in", "ev_in", "t_in"))
        stored = sem("stored")
        ident0, ident_ready = sem("ident0"), sem("ident_ready")
        mhalf_ready, eps_ready = sem("mhalf_ready"), sem("eps_ready")
        negt_ready, exp_ready, coefT_done, coef_ready = map(sem, ("negt_ready", "exp_ready", "coefT_done", "coef_ready"))
        xhi_ready, x_ready = sem("xhi_ready"), sem("x_ready")
        hi1_ready, lo1_ready, mm1_done = sem("hi1_ready"), sem("lo1_ready"), sem("mm1_done")
        spec_out, sT_done, shi_ready, s_ready = map(sem, ("spec_out", "sT_done", "shi_ready", "s_ready"))
        turned, hi_ready, lo_ready, mm_done = map(sem, ("turned", "hi_ready", "lo_ready", "mm_done"))
        acc_out, accT_done = sem("acc_out"), sem("accT_done")
        sum2, st2, halves2, betw2, mv2, ve2, cen2, rs2, x1_ready, x1_kept = map(
            sem, ("sum2", "st2", "halves2", "betw2", "mv2", "ve2", "cen2", "rs2", "x1_ready", "x1_kept"))
        x1T_done, x1T_ready, xw_done, phi_ready, p_ready = map(sem, ("x1T_done", "x1T_ready", "xw_done", "phi_ready", "p_ready"))
        sum3, sum3b, deg_s, deg1_s, rdeg_s, pre3, tanh_ready, y_ready = map(
            sem, ("sum3", "sum3b", "deg_s", "deg1_s", "rdeg_s", "pre3", "tanh_ready", "y_ready"))
        st3, halves3, betw3, mv3, ve3, cen3, rs3, out_ready = map(
            sem, ("st3", "halves3", "betw3", "mv3", "ve3", "cen3", "rs3", "out_ready"))

        block = ctx.enter_context(nc.Block())

        def group(which, e):
            return LAST - e if which == 2 else e - NG

        def loads(which, e):
            return e + NG if which == 2 else e + NG - 1

        def run_visits(eng, visit):
            visit(2, 0, None)
            with eng.Fori(1, NG) as e:
                visit(2, e, 2)
            visit(3, NG, 2)
            with eng.Fori(NG + 1, 2 * NG) as e:
                visit(3, e, 3)

        @block.sync
        def _(sp):
            def load(g, k, freed=None, count=None):
                if freed is not None:
                    sp.compute_val(adj_v[g, k].offset * 4)
                    sp.wait_ge(freed, count)
                sp.dma_start(raw[:, k], adj_v[g, k]).then_inc(raw_in[k], 16)

            sp.dma_start(x_sb[:, 0, :].rearrange("p (j c) -> p j c", c=C), x_v[:, 0:R, :]).then_inc(x_in, 16)
            load(0, 0)
            load(0, 1)
            sp.dma_start(x_sb[:, 1:NG, :].rearrange("p g (j c) -> p (g j) c", c=C),
                         x_v[:, R:N // P, :]).then_inc(x_rest_in, 16)
            for k in range(2, NK):
                load(0, k)
            with sp.Fori(1, NG) as v:
                for k in range(NK):
                    load(v, k, lo1_ready, (v - 1) * NK + (k + 1))
            with sp.Fori(1, NG) as e:
                for k in range(NK):
                    load(group(2, e), k, turned, (e - 1) * PAIRS + (2 * k + 2))
            with sp.Fori(NG + 1, 2 * NG) as e:
                for n, k in enumerate(ORDER[3]):
                    load(group(3, e), k, turned, (e - 1) * PAIRS + (2 * n + 2))

        @block.gpsimd
        def _(pool):
            nc.gpsimd.memset(ident[:, :], 0.0).then_inc(ident0, 1)
            pool.wait_ge(ident0, 1)
            nc.gpsimd.affine_select(out=ident[:, :], in_=ident[:, :], compare_op=ALU.not_equal, fill=1.0,
                                    base=0, pattern=[[-1, P]], channel_multiplier=1).then_inc(ident_ready, 1)
            nc.gpsimd.memset(mhalf[:, :], -0.5).then_inc(mhalf_ready, 1)
            pool.wait_ge(mhalf_ready, 1)

            nc.gpsimd.memset(eps_sb[:, :], EPS).then_inc(eps_ready, 1)
            pool.wait_ge(eps_ready, 1)

            def by_row(a):
                return a.unsqueeze(2).to_broadcast([P, R, C])

            def blocks(a):
                return a.rearrange("p (r c) -> p r c", c=C)

            def normalise(src, n, mv_sem, ve_sem, rs_sem, cen_sem):
                pool.wait_ge(mv_sem, n + 1)
                nc.gpsimd.tensor_tensor(veps[:, :], var[:, :], eps_sb[:, :], ALU.add).then_inc(ve_sem, 1)
                nc.gpsimd.tensor_tensor(blocks(cen_g[:, :]), blocks(src[:, :]), by_row(mean[:, :]),
                                        ALU.subtract).then_inc(cen_sem, 1)
                pool.wait_ge(ve_sem, n + 1)
                nc.gpsimd.tensor_tensor(rstd[:, :], veps[:, :], mhalf[:, :], ALU.pow).then_inc(rs_sem, 1)
                pool.wait_ge(cen_sem, n + 1)
                pool.wait_ge(rs_sem, n + 1)

            def scaled(dst):
                return nc.gpsimd.tensor_tensor(blocks(dst), blocks(cen_g[:, :]), by_row(rstd[:, :]), ALU.mult)

            def end2(n, g):
                if not isinstance(g, int):
                    pool.compute_val(x_sb[:, g, :].offset)
                normalise(h_g, n, mv2, ve2, rs2, cen2)
                scaled(x_sb[:, g, :]).then_inc(x1_kept, 1)
                scaled(x1_g[:, :]).then_inc(x1_ready, 1)

            def end3(n, g):
                pool.wait_ge(x1_kept, NG)
                pool.wait_ge(tanh_ready, n + 1)
                nc.gpsimd.tensor_tensor(y_g[:, :], x_sb[:, g, :], th_g[:, :], ALU.add).then_inc(y_ready, 1)
                normalise(y_g, n, mv3, ve3, rs3, cen3)
                if not (isinstance(n, int) and n == 0):
                    pool.wait_ge(stored, 16 * n)
                scaled(o_g[:, :]).then_inc(out_ready, 1)

            with pool.Fori(0, NG) as n:
                end2(n, LAST - n)
            end3(0, 0)
            with pool.Fori(1, NG) as n:
                end3(n, n)

        @block.scalar
        def _(act):
            act.dma_start(ev[:, :], evals.rearrange("(j p) -> j p", p=P)).then_inc(ev_in, 16)
            act.dma_start(t_bc[:, :], t.rearrange("(a n) -> a n", a=1).to_broadcast([N // P, 1])).then_inc(t_in, 16)
            act.dma_start(w_sb[:, :], W).then_inc(w_in, 16)
            act.dma_start(b_bc[:, :], b.rearrange("(a n) -> a n", a=1).to_broadcast([P, C])).then_inc(b_in, 16)
            act.wait_ge(ev_in, 16)
            act.wait_ge(negt_ready, 1)
            nc.scalar.activation(ex[:, :], ev[:, :], ACT.Exp, scale=neg_t[:, 0:1]).then_inc(exp_ready, 1)

            def split_x(v, par):
                if isinstance(v, int) and v == 0:
                    act.wait_ge(x_in, 16)
                else:
                    act.wait_ge(x_rest_in, 16)
                nc.scalar.activation(xg_hi[:, par, :], x_sb[:, v, :], ACT.Copy).then_inc(xhi_ready, 1)

            def chunk1(v, k):
                s = k % 2
                act.wait_ge(raw_in[k], 16 * v + 16)
                if not (isinstance(v, int) and v == 0 and k < 2):
                    act.wait_ge(mm1_done, NK * v + (k - 1))
                for r in range(R):
                    last = nc.scalar.activation(hi[:, 2 * s + r // 2, (r % 2) * CW:(r % 2 + 1) * CW],
                                                raw[:, k, r, :], ACT.Copy,
                                                accum_out=rsum[:, v, r * NK + k:r * NK + k + 1])
                last.then_inc(hi1_ready, 1)

            def visit1(v, par):
                for k in range(NK):
                    chunk1(v, k)
                    if k == NK // 2:
                        split_x(v + 1, 1 - par)

            split_x(0, 0)
            visit1(0, 0)
            with act.Fori(0, (NG - 2) // 2) as d:
                visit1(2 * d + 1, 1)
                visit1(2 * d + 2, 0)

            for i in range(NK + 4):
                if i < NK:
                    chunk1(LAST, i)
                if 0 <= (k := i - 2) < NK:
                    act.wait_ge(mm1_done, NK * LAST + k + 1)
                    if k >= 2:
                        act.wait_ge(sT_done, k - 1)
                    nc.scalar.activation(stage[:, k % 2, :], ps[:, k, :], ACT.Copy).then_inc(spec_out, 1)
                if 0 <= (k := i - 4) < NK:
                    act.wait_ge(sT_done, k + 1)
                    if k == 0:
                        act.wait_ge(coef_ready, 1)
                    for jj in range(JB):
                        j = k * JB + jj
                        last = nc.scalar.activation(s_hi[:, j * C:(j + 1) * C], ps[:, k, jj * C:(jj + 1) * C],
                                                    ACT.Copy, scale=coef[:, j:j + 1])
                    last.then_inc(shi_ready, 1)

            def acc_to_stage(e):
                act.wait_ge(mm_done, (e + 1) * PAIRS)
                nc.scalar.activation(stage[:, 0, :], acc[:, e % 2, :], ACT.Copy).then_inc(acc_out, 1)

            def ending(which, e, q):
                if q == AT_ACC:
                    acc_to_stage(e)
                if which == 2:
                    n, g = e, group(2, e)
                    if q == AT_X1T_OUT:
                        act.wait_ge(x1T_done, n + 1)
                        nc.scalar.activation(stage[:, 1, :], bank_b, ACT.Copy).then_inc(x1T_ready, 1)
                    if q == AT_P_OUT:
                        act.wait_ge(xw_done, n + 1)
                        nc.scalar.activation(p_hi[:, g, :], bank_a, ACT.Copy).then_inc(phi_ready, 1)
                if which == 3:
                    n, g = e - NG, group(3, e)
                    if q == AT_TANH:
                        act.wait_ge(pre3, n + 1)
                        nc.scalar.activation(th_g[:, :], h_g[:, :], ACT.Tanh).then_inc(tanh_ready, 1)
                    if q == AT_STORE:
                        act.wait_ge(out_ready, n + 1)
                        act.dma_start(out_v[g], o_g[:, :].rearrange("p (r c) -> p r c", c=C)).then_inc(stored, 16)

            def visit(which, e, before):
                for q in range(PAIRS):
                    act.wait_ge(turned, e * PAIRS + q + 1)
                    if before or q >= RING:
                        act.wait_ge(mm_done, e * PAIRS + (q - RING + 1))
                    nc.scalar.activation(hi[:, q % RING, :], ps[:, 2 * (q % 2):2 * (q % 2) + 2, :], ACT.Copy)\
                        .then_inc(hi_ready, 1)
                    if before:
                        ending(before, e - 1, q)

            run_visits(act, visit)
            for q in range(PAIRS):
                ending(3, 2 * NG - 1, q)
            act.wait_ge(stored, 16 * NG)

        @block.vector
        def _(dve):
            dve.wait_ge(t_in, 16)
            nc.vector.tensor_scalar(neg_t[:, :], t_bc[:, :], 1e-8, -1.0, ALU.max, ALU.mult).then_inc(negt_ready, 1)

            def split_x(v, par):
                dve.wait_ge(xhi_ready, v + 1)
                nc.vector.tensor_tensor(xg_lo[:, par, :], x_sb[:, v, :], xg_hi[:, par, :].bitcast(f32),
                                        ALU.subtract).then_inc(x_ready, 1)

            def chunk1(v, k):
                s = k % 2
                dve.wait_ge(hi1_ready, NK * v + k + 1)
                nc.vector.tensor_tensor(lo[:, 2 * s:2 * s + 2, :].rearrange("p a n -> p (a n)"),
                                        raw[:, k, :, :].rearrange("p r n -> p (r n)"),
                                        hi[:, 2 * s:2 * s + 2, :].rearrange("p a n -> p (a n)").bitcast(f32),
                                        ALU.subtract).then_inc(lo1_ready, 1)

            def visit1(v, par):
                for k in range(NK):
                    chunk1(v, k)
                    if k == NK // 2:
                        split_x(v + 1, 1 - par)

            split_x(0, 0)
            chunk1(0, 0)
            dve.wait_ge(coefT_done, 1)
            nc.vector.tensor_copy(coef[:, :], ps[:, NK - 1, 0:N // P]).then_inc(coef_ready, 1)
            for k in range(1, NK):
                chunk1(0, k)
            split_x(1, 1)
            with dve.Fori(0, (NG - 2) // 2) as d:
                visit1(2 * d + 1, 1)
                visit1(2 * d + 2, 0)
            for i in range(NK + 4):
                if i < NK:
                    chunk1(LAST, i)
                if 0 <= (k := i - 4) < NK:
                    dve.wait_ge(shi_ready, k + 1)
                    for jj in range(JB):
                        j = k * JB + jj
                        last = nc.vector.scalar_tensor_tensor(
                            out=s_lo[:, j * C:(j + 1) * C], in0=ps[:, k, jj * C:(jj + 1) * C],
                            scalar=coef[:, j:j + 1], in1=s_hi[:, j * C:(j + 1) * C].bitcast(f32),
                            op0=ALU.mult, op1=ALU.subtract)
                    last.then_inc(s_ready, 1)

            g_before = [None]

            def layer_stats(src, ready, n, st, halves, betw, done):
                dve.wait_ge(ready, n + 1)
                for r in range(R):
                    last = nc.vector.bn_stats(stats[:, r, :], src[:, r * C:(r + 1) * C])
                last.then_inc(st, 1)
                dve.wait_ge(st, n + 1)
                even, odd = stats[:, :, 0:3], stats[:, :, 3:6]
                nc.vector.tensor_tensor(msum[:, :], even[:, :, 1], odd[:, :, 1], ALU.add)
                nc.vector.tensor_tensor(mdif[:, :], even[:, :, 1], odd[:, :, 1], ALU.subtract)
                nc.vector.tensor_tensor(m2[:, :], even[:, :, 2], odd[:, :, 2], ALU.add).then_inc(halves, 1)
                dve.wait_ge(halves, n + 1)
                nc.vector.tensor_scalar(mean[:, :], msum[:, :], 0.5, None, ALU.mult)
                nc.vector.scalar_tensor_tensor(out=between[:, :], in0=mdif[:, :], scalar=0.25, in1=mdif[:, :],
                                               op0=ALU.mult, op1=ALU.mult).then_inc(betw, 1)
                dve.wait_ge(betw, n + 1)
                nc.vector.scalar_tensor_tensor(out=var[:, :], in0=m2[:, :], scalar=1.0 / C, in1=between[:, :],
                                               op0=ALU.mult, op1=ALU.add).then_inc(done, 1)

            def ending(which, e, q):
                if which == 2:
                    n, g = e, g_before[0]
                    if q == AT_SUM:
                        dve.wait_ge(accT_done, e + 1)
                        nc.vector.tensor_tensor(h_g[:, :], bank_a, x_sb[:, g, :], ALU.add).then_inc(sum2, 1)
                        layer_stats(h_g, sum2, n, st2, halves2, betw2, mv2)
                    if q == AT_P_OUT:
                        dve.wait_ge(phi_ready, n + 1)
                        nc.vector.tensor_tensor(p_lo[:, g, :], bank_a, p_hi[:, g, :].bitcast(f32),
                                                ALU.subtract).then_inc(p_ready, 1)
                if which == 3:
                    n, g = e - NG, g_before[0]
                    if q == AT_SUM:
                        dve.wait_ge(accT_done, e + 1)
                        nc.vector.tensor_tensor(h_g[:, :], bank_a, p_hi[:, g, :].bitcast(f32), ALU.add)\
                            .then_inc(sum3, 1)
                        nc.vector.tensor_reduce(deg[:, :], rsum[:, g, :].rearrange("p (r k) -> p r k", k=NK),
                                                mybir.AxisListType.X, ALU.add).then_inc(deg_s, 1)
                        dve.wait_ge(sum3, n + 1)
                        nc.vector.tensor_tensor(h_g[:, :], h_g[:, :], p_lo[:, g, :].bitcast(f32), ALU.add)\
                            .then_inc(sum3b, 1)
                        dve.wait_ge(deg_s, n + 1)
                        nc.vector.tensor_scalar_add(deg1[:, :], deg[:, :], 1.0).then_inc(deg1_s, 1)
                        dve.wait_ge(deg1_s, n + 1)
                        nc.vector.reciprocal(rdeg[:, :], deg1[:, :]).then_inc(rdeg_s, 1)
                        dve.wait_ge(sum3b, n + 1)
                        dve.wait_ge(rdeg_s, n + 1)
                        for r in range(R):
                            last = nc.vector.scalar_tensor_tensor(
                                out=h_g[:, r * C:(r + 1) * C], in0=h_g[:, r * C:(r + 1) * C],
                                scalar=rdeg[:, r:r + 1], in1=b_bc[:, :], op0=ALU.mult, op1=ALU.add)
                        last.then_inc(pre3, 1)
                    if q == AT_STATS3:
                        layer_stats(y_g, y_ready, n, st3, halves3, betw3, mv3)

            def visit(which, e, before):
                if before:
                    g_before[0] = group(before, e - 1)
                    if not isinstance(e, int):
                        dve.compute_val(x_sb[:, g_before[0], :].offset)
                for q in range(PAIRS):
                    dve.wait_ge(hi_ready, e * PAIRS + q + 1)
                    nc.vector.tensor_tensor(lo[:, q % RING, :],
                                            ps[:, 2 * (q % 2):2 * (q % 2) + 2, :].rearrange("p a n -> p (a n)"),
                                            hi[:, q % RING, :].bitcast(f32), ALU.subtract).then_inc(lo_ready, 1)
                    if before:
                        ending(before, e - 1, q)

            dve.wait_ge(x_rest_in, 16)
            dve.wait_ge(b_in, 16)
            run_visits(dve, visit)
            g_before[0] = LAST
            for q in range(PAIRS):
                ending(3, 2 * NG - 1, q)

        @block.tensor
        def _(pe):
            pe.wait_ge(ident_ready, 1)
            pe.wait_ge(exp_ready, 1)
            nc.tensor.transpose(ps[:, NK - 1, 0:N // P], ex[:, :], ident[0:N // P, 0:N // P]).then_inc(coefT_done, 1)

            def chunk1(v, k, par, first, final):
                pe.wait_ge(lo1_ready, NK * v + k + 1)
                s = k % 2
                for r in range(R):
                    xh, xl = (a[:, par, r * C:(r + 1) * C] for a in (xg_hi, xg_lo))
                    ah, al = (a[:, 2 * s + r // 2, (r % 2) * CW:(r % 2 + 1) * CW] for a in (hi, lo))
                    nc.tensor.matmul(ps[:, k, :], xh, ah, start=first and r == 0, stop=False)
                    nc.tensor.matmul(ps[:, k, :], xh, al, start=False, stop=False)
                    last = nc.tensor.matmul(ps[:, k, :], xl, ah, start=False, stop=final and r == R - 1)
                last.then_inc(mm1_done, 1)

            def visit1(v, par, first=False):
                pe.wait_ge(x_ready, v + 1)
                for k in range(NK):
                    if first and k == NK - 1:
                        pe.wait_ge(coef_ready, 1)
                    chunk1(v, k, par, first, False)

            visit1(0, 0, first=True)
            with pe.Fori(0, (NG - 2) // 2) as d:
                visit1(2 * d + 1, 1)
                visit1(2 * d + 2, 0)
            pe.wait_ge(x_ready, NG)
            for i in range(NK + 2):
                if i < NK:
                    chunk1(LAST, i, 1, False, True)
                if 0 <= (k := i - 2) < NK:
                    pe.wait_ge(spec_out, k + 1)
                    for jj in range(JB):
                        last = nc.tensor.transpose(ps[:, k, jj * C:(jj + 1) * C],
                                                   stage[:, k % 2, jj * P:(jj + 1) * P], ident[:, :])
                    last.then_inc(sT_done, 1)

            def turn(which, e, q):
                k = ORDER[which][q // 2]
                if q % 2 == 0:
                    pe.wait_ge(raw_in[k], loads(which, e) * 16)
                for jj in range(2):
                    cols = (2 * (q % 2) + jj) * P
                    for r in range(R):
                        last = nc.tensor.transpose(ps[:, 2 * (q % 2) + jj, r * P:(r + 1) * P],
                                                   raw[:, k, r, cols:cols + P], ident[:, :])
                last.then_inc(turned, 1)

            def products(which, e, q):
                k = ORDER[which][q // 2]
                v_hi, v_lo = (s_hi, s_lo) if which == 2 else \
                    (a[:, :, :].rearrange("p g n -> p (g n)") for a in (p_hi, p_lo))
                out_t = acc[:, e % 2, :]
                for jj in range(2):
                    j = k * JB + 2 * (q % 2) + jj
                    vh, vl = (a[:, j * C:(j + 1) * C] for a in (v_hi, v_lo))
                    ah, al = (a[:, q % RING, jj * CW:(jj + 1) * CW] for a in (hi, lo))
                    nc.tensor.matmul(out_t, vh, ah, start=q == 0 and jj == 0, stop=False)
                    nc.tensor.matmul(out_t, vh, al, start=False, stop=False)
                    last = nc.tensor.matmul(out_t, vl, ah, start=False, stop=q == PAIRS - 1 and jj == 1)
                last.then_inc(mm_done, 1)

            def ending(which, e, q):
                if q == AT_TURN:
                    pe.wait_ge(acc_out, e + 1)
                    for r in range(R):
                        last = nc.tensor.transpose(bank_a[:, r * C:(r + 1) * C], stage[:, 0, r * P:(r + 1) * P],
                                                   ident[:, :])
                    last.then_inc(accT_done, 1)
                if which == 2 and q == AT_X1T:
                    pe.wait_ge(x1_ready, e + 1)
                    for r in range(R):
                        last = nc.tensor.transpose(bank_b[:, r * P:(r + 1) * P], x1_g[:, r * C:(r + 1) * C],
                                                   ident[:, :])
                    last.then_inc(x1T_done, 1)
                if which == 2 and q == AT_P:
                    pe.wait_ge(x1T_ready, e + 1)
                    pe.wait_ge(sum2, e + 1)
                    for r in range(R):
                        last = nc.tensor.matmul(bank_a[:, r * C:(r + 1) * C], stage[:, 1, r * P:(r + 1) * P],
                                                w_sb[:, :], start=True, stop=True)
                    last.then_inc(xw_done, 1)

            def visit(which, e, before):
                for q in range(PAIRS):
                    if before or q >= LAG:
                        pe.wait_ge(lo_ready, e * PAIRS + (q - LAG + 1))
                    elif q < LAG:
                        pe.wait_ge(s_ready, 2 * q + 2)
                    turn(which, e, q)
                    if q >= LAG:
                        k = ORDER[which][(q - LAG) // 2]
                        if q == LAG:
                            if not before:
                                pe.wait_ge(s_ready, 5)
                            if which == 3 and before == 2:
                                pe.wait_ge(p_ready, NG - 1)
                        if not before and (q - LAG) % 2 == 0:
                            pe.wait_ge(s_ready, k + 1)
                        products(which, e, q - LAG)
                    elif before:
                        if which == 3 and q == 0 and before == 3:
                            pe.wait_ge(p_ready, NG)
                        products(before, e - 1, PAIRS + q - LAG)
                    if before:
                        ending(before, e - 1, q)

            pe.wait_ge(w_in, 16)
            run_visits(pe, visit)
            for q in range(PAIRS):
                if q < LAG:
                    pe.wait_ge(lo_ready, 2 * NG * PAIRS + (q - LAG + 1))
                    products(3, 2 * NG - 1, PAIRS + q - LAG)
                ending(3, 2 * NG - 1, q)


_INS = ['x', 'adj', 'L0_gnn_evals', 'L0_gnn_t', 'L1_gnn_W', 'L1_gnn_b']


def kernel(**inputs):
    import numpy as _np
    import concourse.bacc as _bacc
    from concourse import mybir as _mybir
    from concourse.bass_utils import run_bass_kernel_spmd as _run

    nc = _bacc.Bacc("TRN2", target_bir_lowering=False, num_devices=1)
    arrays, args = {}, []
    for name in _INS:
        a = _np.ascontiguousarray(inputs[name])
        arrays[f"in_{name}_dram"] = a
        args.append(nc.dram_tensor(f"in_{name}_dram", a.shape, _mybir.dt.from_np(a.dtype), kind="ExternalInput").ap())
    shape = arrays["in_x_dram"].shape
    args.append(nc.dram_tensor("out_0_dram", shape, _mybir.dt.float32, kind="ExternalOutput").ap())
    spectral_then_graph_conv(nc, *args)
    r = _run(nc, [arrays], core_ids=[0])
    return r.results[0]["out_0_dram"]
```

```python
import concourse.bass as bass
from concourse import mybir
from contextlib import ExitStack


def spectral_then_graph_conv(nc, x, adj, evals, t, W, b, out):
    f32 = mybir.dt.float32
    f32r = mybir.dt.float32r
    ALU = mybir.AluOpType
    ACT = mybir.ActivationFunctionType

    P = 128
    N, C = x.shape
    assert C == P and N % (4 * P) == 0
    R = 4
    CW = 512
    NG = N // (R * P)
    NK = N // CW
    JB = CW // P
    PAIRS = 2 * NK
    TSLOTS = 3
    RING = 4
    LAG = 3
    LAST = NG - 1
    EPS = 1e-5
    QP = 32
    QN = P // QP
    RB = CW // QP
    TURNED_BY_VECTOR = (2, 4, 6)
    assert NG == NK and NG % 2 == 0 and JB == R == QN

    ORDER = {2: list(range(NK)), 3: [1, 3, 2, 5, 4, 7, 6, 0]}
    TURN_AT = {1: 4, 3: 5, 5: 8, 7: 9, 9: 12, 11: 13}

    def by_vector(which, e):
        first = isinstance(e, int) and e == 0
        return [] if first else [q for q in range(PAIRS) if ORDER[which][q // 2] in TURNED_BY_VECTOR]

    def by_tensor(which, e):
        return [q for q in range(PAIRS) if q not in by_vector(which, e)]

    VPAIRS = 2 * len(TURNED_BY_VECTOR)
    TPAIRS = PAIRS - VPAIRS

    def tslot(which, e, q):
        early = by_vector(which, e) and q < by_vector(which, e)[0]
        return (q + (2 if early else 1)) % TSLOTS

    def turned_before(e):
        return 0 if isinstance(e, int) and e == 0 else e * TPAIRS + VPAIRS

    def vturned_before(e):
        return 0 if isinstance(e, int) and e == 0 else e * VPAIRS - VPAIRS

    AT_ACC, AT_TURN, AT_SUM = 3, 5, 6
    AT_X1T, AT_X1T_OUT, AT_P, AT_P_OUT = 11, 12, 13, 14
    AT_TANH, AT_STATS3, AT_STORE = 8, 10, 15

    adj_v = adj.rearrange("(g r p) (k w) -> g k p r w", r=R, p=P, w=CW)
    adj_x = adj.rearrange("(g p r) (k w) -> g k p r w", r=R, p=P, w=CW)
    x_v = x.rearrange("(g p m) c -> p g (m c)", p=P, m=JB)
    out_v = out.rearrange("(g p m) c -> g p (m c)", p=P, m=JB)
    adj_q = adj.rearrange("(g b n) (k q w) -> g k q n b w", b=RB, n=QP, q=QN, w=P)

    def spread(a, m):
        return a.rearrange("p (i m) -> p m i", m=JB)[:, m]

    ctx = ExitStack()
    with ctx:
        def sb(name, shape, dt=f32):
            return ctx.enter_context(nc.sbuf_tensor(name, shape, dt))

        def sem(name):
            return ctx.enter_context(nc.semaphore(name))

        raw = sb("raw", [P, NK, R, CW])
        hi = sb("hi", [P, RING, 2 * CW], f32r)
        lo = sb("lo", [P, RING, 2 * CW], f32r)
        x_sb = sb("x_sb", [P, NG, R * C])
        with nc.sbuf_tensor("xg_hi", [P, 2, R * C], f32r) as xg_hi, nc.sbuf_tensor("xg_lo", [P, 2, R * C], f32r) as xg_lo:
            pass
        vt = sb("vt", [P, 2, 2 * CW])
        s_hi = sb("s_hi", [P, N // P * C], f32r)
        s_lo = sb("s_lo", [P, N // P * C], f32r)
        p_hi = sb("p_hi", [P, NG, R * C], f32r)
        p_lo = sb("p_lo", [P, NG, R * C], f32r)
        stage = sb("stage", [P, 2, CW])
        x1_g = sb("x1_g", [P, R * C])
        h_g = sb("h_g", [P, R * C])
        th_g = sb("th_g", [P, R * C])
        y_g = sb("y_g", [P, R * C])
        o_g = sb("o_g", [P, R * C])
        ident = sb("ident", [P, P])
        w_sb = sb("w_sb", [P, C])
        b_bc = sb("b_bc", [P, C])
        ev = sb("ev", [P, N // P])
        t_bc = sb("t_bc", [P, 1])
        neg_t = sb("neg_t", [P, 1])
        coef = sb("coef", [P, N // P])
        rsum = sb("rsum", [P, NG, R * NK])
        rows = sb("rows", [P, NG, R])
        deg = sb("deg", [P, NG, R])
        rdeg = sb("rdeg", [P, NG, R])
        stats = sb("stats", [P, R, 6])
        msum, mdif, m2, mean, between, var = (sb(n, [P, R]) for n in ("msum", "mdif", "m2", "mean", "between", "var"))
        cen_g = sb("cen_g", [P, R * C])
        eps_sb = sb("eps_sb", [P, R])
        veps = sb("veps", [P, R])
        rstd = sb("rstd", [P, R])
        mhalf = sb("mhalf", [P, R])

        ps = ctx.enter_context(nc.psum_tensor("ps", [P, 8, CW], f32))
        acc = ps[:, 6:8, :]

        raw_in = [sem(f"raw_in{k}") for k in range(NK)]
        x_in, x_rest_in, w_in, b_in, ev_in, t_in = map(sem, ("x_in", "x_rest_in", "w_in", "b_in", "ev_in", "t_in"))
        stored = sem("stored")
        ident0, ident_ready = sem("ident0"), sem("ident_ready")
        mhalf_ready, eps_ready = sem("mhalf_ready"), sem("eps_ready")
        negt_ready, coef_ready = map(sem, ("negt_ready", "coef_ready"))
        xhi_ready, x_ready = sem("xhi_ready"), sem("x_ready")
        hi1_ready, lo1_ready, mm1_done = sem("hi1_ready"), sem("lo1_ready"), sem("mm1_done")
        spec_out, sT_done, shi_ready, s_ready = map(sem, ("spec_out", "sT_done", "shi_ready", "s_ready"))
        turned, vturned, hi_ready, lo_ready, mm_done = map(sem, ("turned", "vturned", "hi_ready", "lo_ready", "mm_done"))

        acc_out, accT_done = sem("acc_out"), sem("accT_done")
        sum2, st2, halves2, betw2, mv2, ve2, cen2, rs2, x1_ready, x1_kept = map(
            sem, ("sum2", "st2", "halves2", "betw2", "mv2", "ve2", "cen2", "rs2", "x1_ready", "x1_kept"))
        x1T_done, x1T_ready, xw_done, phi_ready, p_ready = map(sem, ("x1T_done", "x1T_ready", "xw_done", "phi_ready", "p_ready"))
        sum3, sum3b, deg_s, pre3, tanh_ready, y_ready = map(
            sem, ("sum3", "sum3b", "deg_s", "pre3", "tanh_ready", "y_ready"))
        st3, halves3, betw3, mv3, ve3, cen3, rs3, out_ready = map(
            sem, ("st3", "halves3", "betw3", "mv3", "ve3", "cen3", "rs3", "out_ready"))

        block = ctx.enter_context(nc.Block())

        def group(which, e):
            return LAST - e if which == 2 else e - NG

        def loads(which, e):
            return e + NG if which == 2 else e + NG - 1

        def arrived(which, e, k):
            n = loads(which, e)
            return 16 * n if k not in TURNED_BY_VECTOR else 16 * (NG + QN * (n - NG))

        def run_visits(eng, visit):
            visit(2, 0, None, 0)
            visit(2, 1, 2, 1)
            with eng.Fori(1, NG // 2) as d:
                visit(2, 2 * d, 2, 0)
                visit(2, 2 * d + 1, 2, 1)
            visit(3, NG, 2, 0)
            with eng.Fori(NG // 2, NG - 1) as d:
                visit(3, 2 * d + 1, 3, 1)
                visit(3, 2 * d + 2, 3, 0)
            visit(3, 2 * NG - 1, 3, 1)

        @block.sync
        def _(sp):
            def load(src, k, freed=None, count=None):
                if freed is not None:
                    if not isinstance(src.offset, int):
                        sp.compute_val(src.offset * 4)
                    sp.wait_ge(freed, count)
                sp.dma_start(raw[:, k], src).then_inc(raw_in[k], 16)

            sp.dma_start(x_sb[:, 0, :], x_v[:, 0, :]).then_inc(x_in, 16)
            load(adj_x[0, 0], 0)
            load(adj_x[0, 1], 1)
            sp.dma_start(x_sb[:, 1:NG, :], x_v[:, 1:NG, :]).then_inc(x_rest_in, 16)
            for k in range(2, NK):
                load(adj_x[0, k], k)
            with sp.Fori(1, NG) as v:
                for k in range(NK):
                    load(adj_x[v, k], k, lo1_ready, (v - 1) * PAIRS + (2 * k + 2))
            def load_visit(which, e, first):
                for n, k in enumerate(ORDER[which]):
                    vec = k in TURNED_BY_VECTOR
                    if first:
                        freed, count = turned, 2 * n + 2
                    elif vec:
                        freed, count = vturned, vturned_before(e - 1) + (by_vector(which, e).index(2 * n) + 2)
                    else:
                        freed, count = turned, turned_before(e - 1) + (by_tensor(which, e).index(2 * n) + 2)
                    if not vec:
                        load(adj_v[group(which, e), k], k, freed, count)
                        continue
                    for q in range(QN):
                        if not isinstance(e, int):
                            sp.compute_val(adj_q[group(which, e), k, q].offset * 4)
                        if q == 0:
                            sp.wait_ge(freed, count)
                        sp.dma_start(raw[q * QP:(q + 1) * QP, k].rearrange("p r w -> p (r w)")
                                     .rearrange("p (b w) -> p b w", w=P), adj_q[group(which, e), k, q])\
                            .then_inc(raw_in[k], 16)

            load_visit(2, 1, True)
            with sp.Fori(2, NG) as e:
                load_visit(2, e, False)
            with sp.Fori(NG + 1, 2 * NG) as e:
                load_visit(3, e, False)

        @block.gpsimd
        def _(pool):
            nc.gpsimd.memset(ident[:, :], 0.0).then_inc(ident0, 1)
            pool.wait_ge(ident0, 1)
            nc.gpsimd.affine_select(out=ident[:, :], in_=ident[:, :], compare_op=ALU.not_equal, fill=1.0,
                                    base=0, pattern=[[-1, P]], channel_multiplier=1).then_inc(ident_ready, 1)
            nc.gpsimd.memset(mhalf[:, :], -0.5).then_inc(mhalf_ready, 1)
            pool.wait_ge(mhalf_ready, 1)

            nc.gpsimd.memset(eps_sb[:, :], EPS).then_inc(eps_ready, 1)
            pool.wait_ge(eps_ready, 1)

            def by_row(a):
                return a.unsqueeze(2).to_broadcast([P, R, C])

            def blocks(a):
                return a.rearrange("p (r c) -> p r c", c=C)

            def normalise(src, n, mv_sem, ve_sem, rs_sem, cen_sem):
                pool.wait_ge(mv_sem, n + 1)
                nc.gpsimd.tensor_tensor(veps[:, :], var[:, :], eps_sb[:, :], ALU.add).then_inc(ve_sem, 1)
                nc.gpsimd.tensor_tensor(blocks(cen_g[:, :]), blocks(src[:, :]), by_row(mean[:, :]),
                                        ALU.subtract).then_inc(cen_sem, 1)
                pool.wait_ge(ve_sem, n + 1)
                nc.gpsimd.tensor_tensor(rstd[:, :], veps[:, :], mhalf[:, :], ALU.pow).then_inc(rs_sem, 1)
                pool.wait_ge(cen_sem, n + 1)
                pool.wait_ge(rs_sem, n + 1)

            def scaled(dst):
                return nc.gpsimd.tensor_tensor(blocks(dst), blocks(cen_g[:, :]), by_row(rstd[:, :]), ALU.mult)

            def end2(n, g):
                if not isinstance(g, int):
                    pool.compute_val(x_sb[:, g, :].offset)
                normalise(h_g, n, mv2, ve2, rs2, cen2)
                scaled(x_sb[:, g, :]).then_inc(x1_kept, 1)
                scaled(x1_g[:, :]).then_inc(x1_ready, 1)

            def end3(n, g):
                pool.wait_ge(x1_kept, NG)
                pool.wait_ge(tanh_ready, n + 1)
                nc.gpsimd.tensor_tensor(y_g[:, :], x_sb[:, g, :], th_g[:, :], ALU.add).then_inc(y_ready, 1)
                normalise(y_g, n, mv3, ve3, rs3, cen3)
                if not (isinstance(n, int) and n == 0):
                    pool.wait_ge(stored, 16 * n)
                scaled(o_g[:, :]).then_inc(out_ready, 1)

            with pool.Fori(0, NG) as n:
                end2(n, LAST - n)
            end3(0, 0)
            with pool.Fori(1, NG) as n:
                end3(n, n)

        @block.scalar
        def _(act):
            act.dma_start(t_bc[:, :], t.rearrange("(a n) -> a n", a=1).to_broadcast([P, 1])).then_inc(t_in, 16)
            act.dma_start(ev[:, :].rearrange("p (k m) -> p k m", m=JB),
                          evals.rearrange("(k p m) -> p k m", p=P, m=JB)).then_inc(ev_in, 16)
            act.dma_start(w_sb[:, :], W).then_inc(w_in, 16)
            act.dma_start(b_bc[:, :], b.rearrange("(a n) -> a n", a=1).to_broadcast([P, C])).then_inc(b_in, 16)
            act.wait_ge(ev_in, 16)
            act.wait_ge(negt_ready, 1)
            nc.scalar.activation(coef[:, :], ev[:, :], ACT.Exp, scale=neg_t[:, 0:1]).then_inc(coef_ready, 1)

            def split_x(v, par):
                if isinstance(v, int) and v == 0:
                    act.wait_ge(x_in, 16)
                else:
                    act.wait_ge(x_rest_in, 16)
                nc.scalar.activation(xg_hi[:, par, :], x_sb[:, v, :], ACT.Copy).then_inc(xhi_ready, 1)

            def chunk1(v, k):
                act.wait_ge(raw_in[k], 16 * v + 16)
                for h in range(2):
                    q = 2 * k + h
                    if not (isinstance(v, int) and v == 0 and q < RING):
                        act.wait_ge(mm1_done, PAIRS * v + (q - RING + 1))
                    for r in (2 * h, 2 * h + 1):
                        last = nc.scalar.activation(hi[:, q % RING, (r % 2) * CW:(r % 2 + 1) * CW],
                                                    raw[:, k, r, :], ACT.Copy,
                                                    accum_out=rsum[:, v, r * NK + k:r * NK + k + 1])
                    last.then_inc(hi1_ready, 1)

            def visit1(v, par):
                for k in range(NK):
                    chunk1(v, k)
                    if k == NK // 2:
                        split_x(v + 1, 1 - par)

            split_x(0, 0)
            visit1(0, 0)
            with act.Fori(0, (NG - 2) // 2) as d:
                visit1(2 * d + 1, 1)
                visit1(2 * d + 2, 0)

            for i in range(NK + 4):
                if i < NK:
                    chunk1(LAST, i)
                if 0 <= (k := i - 2) < NK:
                    act.wait_ge(mm1_done, PAIRS * LAST + 2 * k + 2)
                    if k >= 2:
                        act.wait_ge(sT_done, k - 1)
                    nc.scalar.activation(stage[:, k % 2, :], ps[:, k, :], ACT.Copy).then_inc(spec_out, 1)
                if 0 <= (k := i - 4) < NK:
                    act.wait_ge(sT_done, k + 1)
                    if k == 0:
                        act.wait_ge(coef_ready, 1)
                    for jj in range(JB):
                        j = k * JB + jj
                        last = nc.scalar.activation(s_hi[:, j * C:(j + 1) * C], ps[:, k, jj * C:(jj + 1) * C],
                                                    ACT.Copy, scale=coef[:, j:j + 1])
                    last.then_inc(shi_ready, 1)

            def acc_to_stage(e, par):
                act.wait_ge(mm_done, (e + 1) * PAIRS)
                nc.scalar.activation(stage[:, 0, :], acc[:, par, :], ACT.Copy).then_inc(acc_out, 1)

            def ending(which, e, q, par):
                if q == AT_ACC:
                    acc_to_stage(e, par)
                if which == 2:
                    n, g = e, group(2, e)
                    if q == AT_X1T_OUT:
                        act.wait_ge(x1T_done, n + 1)
                        nc.scalar.activation(stage[:, 1, :], acc[:, par, :], ACT.Copy).then_inc(x1T_ready, 1)
                    if q == AT_P_OUT:
                        act.wait_ge(xw_done, n + 1)
                        nc.scalar.activation(p_hi[:, g, :], acc[:, par, :], ACT.Copy).then_inc(phi_ready, 1)
                if which == 3:
                    n, g = e - NG, group(3, e)
                    if q == AT_TANH:
                        act.wait_ge(pre3, n + 1)
                        nc.scalar.activation(th_g[:, :], h_g[:, :], ACT.Tanh).then_inc(tanh_ready, 1)
                    if q == AT_STORE:
                        act.wait_ge(out_ready, n + 1)
                        act.dma_start(out_v[g], o_g[:, :]).then_inc(stored, 16)

            def visit(which, e, before, par):
                vec, ten = by_vector(which, e), by_tensor(which, e)
                for q in range(PAIRS):
                    if q in vec:
                        act.wait_ge(vturned, vturned_before(e) + (vec.index(q) + 1))
                        src = vt[:, vec.index(q) % 2, :]
                    else:
                        act.wait_ge(turned, turned_before(e) + (ten.index(q) + 1))
                        slot = tslot(which, e, q)
                        src = ps[:, 2 * slot:2 * slot + 2, :]
                    if before or q >= RING:
                        act.wait_ge(mm_done, e * PAIRS + (q - RING + 1))
                    nc.scalar.activation(hi[:, q % RING, :], src, ACT.Copy)\
                        .then_inc(hi_ready, 1)
                    if before:
                        ending(before, e - 1, q, 1 - par)

            run_visits(act, visit)
            for q in range(PAIRS):
                ending(3, 2 * NG - 1, q, 1)
            act.wait_ge(stored, 16 * NG)

        @block.vector
        def _(dve):
            dve.wait_ge(t_in, 16)
            nc.vector.tensor_scalar(neg_t[:, :], t_bc[:, :], 1e-8, -1.0, ALU.max, ALU.mult).then_inc(negt_ready, 1)

            def split_x(v, par):
                dve.wait_ge(xhi_ready, v + 1)
                nc.vector.tensor_tensor(xg_lo[:, par, :], x_sb[:, v, :], xg_hi[:, par, :].bitcast(f32),
                                        ALU.subtract).then_inc(x_ready, 1)

            def chunk1(v, k):
                for h in range(2):
                    q = 2 * k + h
                    dve.wait_ge(hi1_ready, PAIRS * v + (q + 1))
                    nc.vector.tensor_tensor(lo[:, q % RING, :],
                                            raw[:, k, 2 * h:2 * h + 2, :].rearrange("p r n -> p (r n)"),
                                            hi[:, q % RING, :].bitcast(f32), ALU.subtract).then_inc(lo1_ready, 1)

            def visit1(v, par):
                for k in range(NK):
                    chunk1(v, k)
                    if k == NK // 2:
                        split_x(v + 1, 1 - par)

            split_x(0, 0)
            for k in range(NK):
                chunk1(0, k)
            split_x(1, 1)
            with dve.Fori(0, (NG - 2) // 2) as d:
                visit1(2 * d + 1, 1)
                visit1(2 * d + 2, 0)
            for i in range(NK + 4):
                if i < NK:
                    chunk1(LAST, i)
                if 0 <= (k := i - 4) < NK:
                    dve.wait_ge(shi_ready, k + 1)
                    for jj in range(JB):
                        j = k * JB + jj
                        last = nc.vector.scalar_tensor_tensor(
                            out=s_lo[:, j * C:(j + 1) * C], in0=ps[:, k, jj * C:(jj + 1) * C],
                            scalar=coef[:, j:j + 1], in1=s_hi[:, j * C:(j + 1) * C].bitcast(f32),
                            op0=ALU.mult, op1=ALU.subtract)
                    last.then_inc(s_ready, 1)

            g_before = [None]

            def layer_stats(src, ready, n, st, halves, betw, done):
                dve.wait_ge(ready, n + 1)
                for r in range(R):
                    last = nc.vector.bn_stats(stats[:, r, :], src[:, r * C:(r + 1) * C])
                last.then_inc(st, 1)
                dve.wait_ge(st, n + 1)
                even, odd = stats[:, :, 0:3], stats[:, :, 3:6]
                nc.vector.tensor_tensor(msum[:, :], even[:, :, 1], odd[:, :, 1], ALU.add)
                nc.vector.tensor_tensor(mdif[:, :], even[:, :, 1], odd[:, :, 1], ALU.subtract)
                nc.vector.tensor_tensor(m2[:, :], even[:, :, 2], odd[:, :, 2], ALU.add).then_inc(halves, 1)
                dve.wait_ge(halves, n + 1)
                nc.vector.tensor_scalar(mean[:, :], msum[:, :], 0.5, None, ALU.mult)
                nc.vector.scalar_tensor_tensor(out=between[:, :], in0=mdif[:, :], scalar=0.25, in1=mdif[:, :],
                                               op0=ALU.mult, op1=ALU.mult).then_inc(betw, 1)
                dve.wait_ge(betw, n + 1)
                nc.vector.scalar_tensor_tensor(out=var[:, :], in0=m2[:, :], scalar=1.0 / C, in1=between[:, :],
                                               op0=ALU.mult, op1=ALU.add).then_inc(done, 1)

            def ending(which, e, q, par):
                if which == 2:
                    n, g = e, g_before[0]
                    if q == AT_SUM:
                        dve.wait_ge(accT_done, e + 1)
                        nc.vector.tensor_tensor(h_g[:, :], acc[:, par, :], x_sb[:, g, :], ALU.add).then_inc(sum2, 1)
                        layer_stats(h_g, sum2, n, st2, halves2, betw2, mv2)
                    if q == AT_P_OUT:
                        dve.wait_ge(phi_ready, n + 1)
                        nc.vector.tensor_tensor(p_lo[:, g, :], acc[:, par, :], p_hi[:, g, :].bitcast(f32),
                                                ALU.subtract).then_inc(p_ready, 1)
                if which == 3:
                    n, g = e - NG, g_before[0]
                    if q == AT_SUM:
                        dve.wait_ge(accT_done, e + 1)
                        nc.vector.tensor_tensor(h_g[:, :], acc[:, par, :], p_hi[:, g, :].bitcast(f32), ALU.add)\
                            .then_inc(sum3, 1)
                        dve.wait_ge(sum3, n + 1)
                        nc.vector.tensor_tensor(h_g[:, :], h_g[:, :], p_lo[:, g, :].bitcast(f32), ALU.add)\
                            .then_inc(sum3b, 1)
                        dve.wait_ge(sum3b, n + 1)
                        for r in range(R):
                            last = nc.vector.scalar_tensor_tensor(
                                out=h_g[:, r * C:(r + 1) * C], in0=h_g[:, r * C:(r + 1) * C],
                                scalar=rdeg[:, g, r:r + 1], in1=b_bc[:, :], op0=ALU.mult, op1=ALU.add)
                        last.then_inc(pre3, 1)
                    if q == AT_STATS3:
                        layer_stats(y_g, y_ready, n, st3, halves3, betw3, mv3)

            def visit(which, e, before, par):
                if before:
                    g_before[0] = group(before, e - 1)
                    if not isinstance(e, int):
                        dve.compute_val(x_sb[:, g_before[0], :].offset)
                vec, ten = by_vector(which, e), by_tensor(which, e)
                for q in range(PAIRS):
                    if q in vec:
                        src = vt[:, vec.index(q) % 2, :]
                    else:
                        slot = tslot(which, e, q)
                        src = ps[:, 2 * slot:2 * slot + 2, :].rearrange("p a n -> p (a n)")
                    dve.wait_ge(hi_ready, e * PAIRS + q + 1)
                    nc.vector.tensor_tensor(lo[:, q % RING, :], src,
                                            hi[:, q % RING, :].bitcast(f32), ALU.subtract).then_inc(lo_ready, 1)
                    if vec and q in TURN_AT:
                        turn(which, e, TURN_AT[q], vec.index(TURN_AT[q]))
                    if not before and q == AT_SUM:
                        degrees()
                    if before:
                        ending(before, e - 1, q, 1 - par)

            def degrees():
                nc.vector.tensor_reduce(rows[:, :, :], rsum[:, :, :].rearrange("p g (r k) -> p (g r) k", k=NK),
                                        mybir.AxisListType.X, ALU.add).then_inc(deg_s, 1)
                dve.wait_ge(deg_s, 1)
                nc.vector.tensor_scalar_add(deg[:, :, :], rows[:, :, :], 1.0).then_inc(deg_s, 1)
                dve.wait_ge(deg_s, 2)
                nc.vector.reciprocal(rdeg[:, :, :], deg[:, :, :]).then_inc(deg_s, 1)
                dve.wait_ge(deg_s, 3)

            def turn(which, e, q, n):
                k = ORDER[which][q // 2]
                dve.wait_ge(raw_in[k], arrived(which, e, k))
                if n >= 2:
                    dve.wait_ge(lo_ready, e * PAIRS + (by_vector(which, e)[n - 2] + 1))
                m = 2 * (q % 2)
                nc.vector.transpose(
                    vt[:, n % 2, :].rearrange("p (m b i) -> p m b i", m=2, b=RB),
                    raw[:, k].rearrange("p r w -> p (r w)").rearrange("p (b i m) -> p m b i", b=RB, m=JB)[:, m:m + 2])\
                    .then_inc(vturned, 1)

            dve.wait_ge(x_rest_in, 16)
            dve.wait_ge(b_in, 16)
            run_visits(dve, visit)
            g_before[0] = LAST
            for q in range(PAIRS):
                ending(3, 2 * NG - 1, q, 1)

        @block.tensor
        def _(pe):
            pe.wait_ge(ident_ready, 1)

            def chunk1(v, k, par, first, final):
                for h in range(2):
                    q = 2 * k + h
                    pe.wait_ge(lo1_ready, PAIRS * v + (q + 1))
                    for r in (2 * h, 2 * h + 1):
                        xh, xl = (a[:, par, r * C:(r + 1) * C] for a in (xg_hi, xg_lo))
                        ah, al = (a[:, q % RING, (r % 2) * CW:(r % 2 + 1) * CW] for a in (hi, lo))
                        nc.tensor.matmul(ps[:, k, :], xh, ah, start=first and r == 0, stop=False)
                        nc.tensor.matmul(ps[:, k, :], xh, al, start=False, stop=False)
                        last = nc.tensor.matmul(ps[:, k, :], xl, ah, start=False, stop=final and r == R - 1)
                    last.then_inc(mm1_done, 1)

            def visit1(v, par, first=False):
                pe.wait_ge(x_ready, v + 1)
                for k in range(NK):
                    chunk1(v, k, par, first, False)

            visit1(0, 0, first=True)
            with pe.Fori(0, (NG - 2) // 2) as d:
                visit1(2 * d + 1, 1)
                visit1(2 * d + 2, 0)
            pe.wait_ge(x_ready, NG)
            for i in range(NK + 2):
                if i < NK:
                    chunk1(LAST, i, 1, False, True)
                if 0 <= (k := i - 2) < NK:
                    pe.wait_ge(spec_out, k + 1)
                    for jj in range(JB):
                        last = nc.tensor.transpose(ps[:, k, jj * C:(jj + 1) * C],
                                                   spread(stage[:, k % 2, :], jj), ident[:, :])
                    last.then_inc(sT_done, 1)

            def turn(which, e, q):
                k = ORDER[which][q // 2]
                if q % 2 == 0:
                    pe.wait_ge(raw_in[k], arrived(which, e, k))
                for jj in range(2):
                    for r in range(R):
                        last = nc.tensor.transpose(ps[:, 2 * tslot(which, e, q) + jj, r * P:(r + 1) * P],
                                                   spread(raw[:, k, r, :], 2 * (q % 2) + jj), ident[:, :])
                last.then_inc(turned, 1)

            def products(which, e, q, par):
                k = ORDER[which][q // 2]
                v_hi, v_lo = (s_hi, s_lo) if which == 2 else \
                    (a[:, :, :].rearrange("p g n -> p (g n)") for a in (p_hi, p_lo))
                out_t = acc[:, par, :]
                for jj in range(2):
                    j = k * JB + 2 * (q % 2) + jj
                    vh, vl = (a[:, j * C:(j + 1) * C] for a in (v_hi, v_lo))
                    ah, al = (a[:, q % RING, jj * CW:(jj + 1) * CW] for a in (hi, lo))
                    nc.tensor.matmul(out_t, vh, ah, start=q == 0 and jj == 0, stop=False)
                    nc.tensor.matmul(out_t, vh, al, start=False, stop=False)
                    last = nc.tensor.matmul(out_t, vl, ah, start=False, stop=q == PAIRS - 1 and jj == 1)
                last.then_inc(mm_done, 1)

            def ending(which, e, q, par):
                bank = acc[:, par, :]
                if q == AT_TURN:
                    pe.wait_ge(acc_out, e + 1)
                    for r in range(R):
                        rows_r = stage[:, 0, r * P:(r + 1) * P] if isinstance(e, int) and e == 0 \
                            else spread(stage[:, 0, :], r)
                        last = nc.tensor.transpose(bank[:, r * C:(r + 1) * C], rows_r, ident[:, :])
                    last.then_inc(accT_done, 1)
                if which == 2 and q == AT_X1T:
                    pe.wait_ge(x1_ready, e + 1)
                    for r in range(R):
                        last = nc.tensor.transpose(bank[:, r * P:(r + 1) * P], x1_g[:, r * C:(r + 1) * C],
                                                   ident[:, :])
                    last.then_inc(x1T_done, 1)
                if which == 2 and q == AT_P:
                    pe.wait_ge(x1T_ready, e + 1)
                    for r in range(R):
                        last = nc.tensor.matmul(bank[:, r * C:(r + 1) * C], stage[:, 1, r * P:(r + 1) * P],
                                                w_sb[:, :], start=True, stop=True)
                    last.then_inc(xw_done, 1)

            def visit(which, e, before, par):
                ten = by_tensor(which, e)
                for q in range(PAIRS):
                    if before or q >= LAG:
                        pe.wait_ge(lo_ready, e * PAIRS + (q - LAG + 1))
                    else:
                        pe.wait_ge(s_ready, 2 * tslot(which, e, q) + 2)
                    if q in ten:
                        turn(which, e, q)
                    if q >= LAG:
                        if q == LAG:
                            if not before:
                                pe.wait_ge(s_ready, NK)
                            if which == 3 and before == 2:
                                pe.wait_ge(p_ready, NG - 1)
                        products(which, e, q - LAG, par)
                    elif before:
                        if which == 3 and q == 0 and before == 3:
                            pe.wait_ge(p_ready, NG)
                        products(before, e - 1, PAIRS + q - LAG, 1 - par)
                    if before:
                        ending(before, e - 1, q, 1 - par)

            pe.wait_ge(w_in, 16)
            run_visits(pe, visit)
            for q in range(PAIRS):
                if q < LAG:
                    pe.wait_ge(lo_ready, 2 * NG * PAIRS + (q - LAG + 1))
                    products(3, 2 * NG - 1, PAIRS + q - LAG, 1)
                ending(3, 2 * NG - 1, q, 1)


_INS = ['x', 'adj', 'L0_gnn_evals', 'L0_gnn_t', 'L1_gnn_W', 'L1_gnn_b']


def kernel(**inputs):
    import numpy as _np
    import concourse.bacc as _bacc
    from concourse import mybir as _mybir
    from concourse.bass_utils import run_bass_kernel_spmd as _run

    nc = _bacc.Bacc("TRN2", target_bir_lowering=False, num_devices=1)
    arrays, args = {}, []
    for name in _INS:
        a = _np.ascontiguousarray(inputs[name])
        arrays[f"in_{name}_dram"] = a
        args.append(nc.dram_tensor(f"in_{name}_dram", a.shape, _mybir.dt.from_np(a.dtype), kind="ExternalInput").ap())
    shape = arrays["in_x_dram"].shape
    args.append(nc.dram_tensor("out_0_dram", shape, _mybir.dt.float32, kind="ExternalOutput").ap())
    spectral_then_graph_conv(nc, *args)
    r = _run(nc, [arrays], core_ids=[0])
    return r.results[0]["out_0_dram"]
```

```python
import concourse.bass as bass
from concourse import mybir
from contextlib import ExitStack


def spectral_then_graph_conv(nc, x, adj, evals, t, W, b, out):
    f32 = mybir.dt.float32
    f32r = mybir.dt.float32r
    ALU = mybir.AluOpType
    ACT = mybir.ActivationFunctionType

    P = 128
    N, C = x.shape
    assert C == P and N % (4 * P) == 0
    R = 4
    CW = 512
    NG = N // (R * P)
    NK = N // CW
    JB = CW // P
    PAIRS = 2 * NK
    TSLOTS = 3
    RING = 4
    LAG = 3
    LAST = NG - 1
    EPS = 1e-5
    QP = 32
    QN = P // QP
    RB = CW // QP
    assert NG == NK and NG % 2 == 0 and JB == R == QN

    PAIR_AT = [(1, 0), (1, 1), (2, 0), (2, 1), (4, 0), (3, 0), (3, 1), (4, 1),
               (5, 0), (5, 1), (7, 0), (6, 0), (6, 1), (7, 1), (0, 0), (0, 1)]
    LOAD_ORDER = [1, 2, 3, 4, 5, 6, 7, 0]
    TURNED_BY_VECTOR = (2, 3, 5, 6, 0)
    LAST_STEP = {k: max(q for q in range(PAIRS) if PAIR_AT[q][0] == k) for k in range(NK)}
    VEC = [q for q in range(PAIRS) if PAIR_AT[q][0] in TURNED_BY_VECTOR]
    POOL_COLS = {2: 0, 3: 1024, 5: 1024, 6: 1024, 8: 0, 9: 1024, 11: 0, 12: 0, 14: 896, 15: 256}
    POOL_LO = [q for q in VEC if POOL_COLS[q] > 0]
    DVE_LO = [q for q in range(PAIRS) if POOL_COLS.get(q, 0) < 2 * CW]

    def is_first(e):
        return isinstance(e, int) and e == 0

    def by_vector(e):
        return [] if is_first(e) else VEC

    def by_tensor(e):
        return [q for q in range(PAIRS) if q not in by_vector(e)]

    def pool_cols(e, q):
        return 0 if is_first(e) else POOL_COLS.get(q, 0)

    VPAIRS = len(VEC)
    TPAIRS = PAIRS - VPAIRS
    assert TPAIRS % TSLOTS == 0 and VPAIRS % 2 == 0

    def tslot(e, q):
        return (q + 2) % TSLOTS if is_first(e) else by_tensor(e).index(q) % TSLOTS

    def turned_by(e, q):
        return (0 if is_first(e) else e * TPAIRS + VPAIRS) + (by_tensor(e).index(q) + 1)

    def vturned_by(e, q):
        return e * VPAIRS - VPAIRS + (VEC.index(q) + 1)

    def pool_lo_by(e, q):
        return e * len(POOL_LO) + (POOL_LO.index(q) + 1 - len(POOL_LO))

    def lo_by(e, q):
        return q + 1 if is_first(e) else e * len(DVE_LO) + (PAIRS - len(DVE_LO) + DVE_LO.index(q) + 1)

    TURN_AT = {2: 0, 3: 1, 5: 3, 6: 4, 8: 6, 9: 7, 11: 9, 12: 10, 14: 12, 15: 13}
    AT_ACC = 2
    AT_TURN = 4
    AT_SUM = 4
    AT_SCALE = 5
    AT_STATS2 = 5
    AT_HALVES2 = 5
    AT_MEAN2 = 5
    AT_VAR2 = 5
    AT_NORM2 = 7
    AT_X1 = 8
    AT_X1_KEPT = 13
    AT_X1T = 11
    AT_X1T_OUT = 12
    AT_P = 13
    AT_P_OUT = 14
    AT_TANH = 8
    AT_Y = 9
    AT_STATS3 = 11
    AT_HALVES3 = 11
    AT_MEAN3 = 11
    AT_VAR3 = 11
    AT_NORM3 = 10
    AT_OUT = 13
    AT_STORE = 15
    AT_P_WHOLE = 0
    adj_v = adj.rearrange("(g r p) (k w) -> g k p r w", r=R, p=P, w=CW)
    adj_x = adj.rearrange("(g p r) (k w) -> g k p r w", r=R, p=P, w=CW)
    x_v = x.rearrange("(g p m) c -> p g (m c)", p=P, m=JB)
    out_v = out.rearrange("(g p m) c -> g p (m c)", p=P, m=JB)
    adj_q = adj.rearrange("(g b n) (k q w) -> g k q n b w", b=RB, n=QP, q=QN, w=P)

    def spread(a, m):
        return a.rearrange("p (i m) -> p m i", m=JB)[:, m]

    ctx = ExitStack()
    with ctx:
        def sb(name, shape, dt=f32):
            return ctx.enter_context(nc.sbuf_tensor(name, shape, dt))

        def sem(name):
            return ctx.enter_context(nc.semaphore(name))

        raw = sb("raw", [P, NK, R, CW])
        hi = sb("hi", [P, RING, 2 * CW], f32r)
        lo = sb("lo", [P, RING, 2 * CW], f32r)
        x_sb = sb("x_sb", [P, NG, R * C])
        with nc.sbuf_tensor("xg_hi", [P, 2, R * C], f32r) as xg_hi, nc.sbuf_tensor("xg_lo", [P, 2, R * C], f32r) as xg_lo:
            pass
        vt = sb("vt", [P, 2, 2 * CW])
        s_hi = sb("s_hi", [P, N // P * C], f32r)
        s_lo = sb("s_lo", [P, N // P * C], f32r)
        p_hi = sb("p_hi", [P, NG, R * C], f32r)
        p_lo = sb("p_lo", [P, NG, R * C], f32r)
        stage = sb("stage", [P, 2, CW])
        x1_g = sb("x1_g", [P, R * C])
        h_g = sb("h_g", [P, R * C])
        p_g = sb("p_g", [P, R * C])
        th_g = sb("th_g", [P, R * C])
        y_g = sb("y_g", [P, R * C])
        o_g = sb("o_g", [P, R * C])
        ident = sb("ident", [P, P])
        w_sb = sb("w_sb", [P, C])
        b_bc = sb("b_bc", [P, C])
        ev = sb("ev", [P, N // P])
        t_bc = sb("t_bc", [P, 1])
        neg_t = sb("neg_t", [P, 1])
        coef = sb("coef", [P, N // P])
        rsum = sb("rsum", [P, NG, R * NK])
        rows = sb("rows", [P, NG, R])
        deg = sb("deg", [P, NG, R])
        rdeg = sb("rdeg", [P, NG, R])
        stats = sb("stats", [P, R, 6])
        msum, mdif, m2, mean, between, var = (sb(n, [P, R]) for n in ("msum", "mdif", "m2", "mean", "between", "var"))
        cen_g = sb("cen_g", [P, R * C])
        eps_sb = sb("eps_sb", [P, R])
        veps = sb("veps", [P, R])
        rstd = sb("rstd", [P, R])
        mhalf = sb("mhalf", [P, R])

        ps = ctx.enter_context(nc.psum_tensor("ps", [P, 8, CW], f32))
        acc = ps[:, 6:8, :]

        raw_in = [sem(f"raw_in{k}") for k in range(NK)]
        x_in, x_rest_in, w_in, b_in, ev_in, t_in = map(sem, ("x_in", "x_rest_in", "w_in", "b_in", "ev_in", "t_in"))
        stored = sem("stored")
        ident0, ident_ready = sem("ident0"), sem("ident_ready")
        mhalf_ready, eps_ready = sem("mhalf_ready"), sem("eps_ready")
        negt_ready, coef_ready = map(sem, ("negt_ready", "coef_ready"))
        xhi_ready, x_ready = sem("xhi_ready"), sem("x_ready")
        hi1_ready, lo1_ready, mm1_done = sem("hi1_ready"), sem("lo1_ready"), sem("mm1_done")
        pool_lo1_ready = sem("pool_lo1_ready")
        spec_out, sT_done, shi_ready, s_ready = map(sem, ("spec_out", "sT_done", "shi_ready", "s_ready"))
        turned, vturned, hi_ready, mm_done = map(sem, ("turned", "vturned", "hi_ready", "mm_done"))
        lo_ready, pool_lo_ready = sem("lo_ready"), sem("pool_lo_ready")

        def wait_lo(eng, e, q):
            if pool_cols(e, q) < 2 * CW:
                eng.wait_ge(lo_ready, lo_by(e, q))
            if pool_cols(e, q) > 0:
                eng.wait_ge(pool_lo_ready, pool_lo_by(e, q))

        acc_out, accT_done = sem("acc_out"), sem("accT_done")
        sum2, st2, halves2, betw2, mv2, ve2, cen2, rs2, x1_ready, x1_kept = map(
            sem, ("sum2", "st2", "halves2", "betw2", "mv2", "ve2", "cen2", "rs2", "x1_ready", "x1_kept"))
        x1T_done, x1T_ready, xw_done, phi_ready, p_ready = map(sem, ("x1T_done", "x1T_ready", "xw_done", "phi_ready", "p_ready"))
        p_whole, sum3, deg_s, pre3, tanh_ready, y_ready = map(
            sem, ("p_whole", "sum3", "deg_s", "pre3", "tanh_ready", "y_ready"))
        st3, halves3, betw3, mv3, ve3, cen3, rs3, out_ready = map(
            sem, ("st3", "halves3", "betw3", "mv3", "ve3", "cen3", "rs3", "out_ready"))

        block = ctx.enter_context(nc.Block())

        def group(which, e):
            return LAST - e if which == 2 else e - NG

        def loads(which, e):
            return e + NG if which == 2 else e + NG - 1

        def arrived(which, e, k):
            n = loads(which, e)
            return 16 * n if k not in TURNED_BY_VECTOR else 16 * (NG + QN * (n - NG))

        def run_visits(eng, visit):
            visit(2, 0, None, 0)
            visit(2, 1, 2, 1)
            with eng.Fori(1, NG // 2) as d:
                visit(2, 2 * d, 2, 0)
                visit(2, 2 * d + 1, 2, 1)
            visit(3, NG, 2, 0)
            with eng.Fori(NG // 2, NG - 1) as d:
                visit(3, 2 * d + 1, 3, 1)
                visit(3, 2 * d + 2, 3, 0)
            visit(3, 2 * NG - 1, 3, 1)

        @block.sync
        def _(sp):
            def load(src, k, freed=None, count=None):
                if freed is not None:
                    if not isinstance(src.offset, int):
                        sp.compute_val(src.offset * 4)
                    sp.wait_ge(freed, count)
                sp.dma_start(raw[:, k], src).then_inc(raw_in[k], 16)

            sp.dma_start(x_sb[:, 0, :], x_v[:, 0, :]).then_inc(x_in, 16)
            load(adj_x[0, 0], 0)
            load(adj_x[0, 1], 1)
            sp.dma_start(x_sb[:, 1:NG, :], x_v[:, 1:NG, :]).then_inc(x_rest_in, 16)
            for k in range(2, NK):
                load(adj_x[0, k], k)
            with sp.Fori(1, NG) as v:
                for k in range(NK):
                    load(adj_x[v, k], k, lo1_ready, (v - 1) * PAIRS + (2 * k + 2))

            def load_visit(which, e):
                for k in LOAD_ORDER:
                    q = LAST_STEP[k]
                    freed, count = (vturned, vturned_by(e - 1, q)) if q in by_vector(e - 1) \
                        else (turned, turned_by(e - 1, q))
                    if k not in TURNED_BY_VECTOR:
                        load(adj_v[group(which, e), k], k, freed, count)
                        continue
                    for qd in range(QN):
                        if not isinstance(e, int):
                            sp.compute_val(adj_q[group(which, e), k, qd].offset * 4)
                        if qd == 0:
                            sp.wait_ge(freed, count)
                        sp.dma_start(raw[qd * QP:(qd + 1) * QP, k].rearrange("p r w -> p (r w)")
                                     .rearrange("p (b w) -> p b w", w=P), adj_q[group(which, e), k, qd])\
                            .then_inc(raw_in[k], 16)

            load_visit(2, 1)
            with sp.Fori(2, NG) as e:
                load_visit(2, e)
            with sp.Fori(NG + 1, 2 * NG) as e:
                load_visit(3, e)

        @block.gpsimd
        def _(pool):
            nc.gpsimd.memset(ident[:, :], 0.0).then_inc(ident0, 1)
            pool.wait_ge(ident0, 1)
            nc.gpsimd.affine_select(out=ident[:, :], in_=ident[:, :], compare_op=ALU.not_equal, fill=1.0,
                                    base=0, pattern=[[-1, P]], channel_multiplier=1).then_inc(ident_ready, 1)
            nc.gpsimd.memset(mhalf[:, :], -0.5).then_inc(mhalf_ready, 1)
            pool.wait_ge(mhalf_ready, 1)

            nc.gpsimd.memset(eps_sb[:, :], EPS).then_inc(eps_ready, 1)
            pool.wait_ge(eps_ready, 1)

            def by_row(a):
                return a.unsqueeze(2).to_broadcast([P, R, C])

            def blocks(a):
                return a.rearrange("p (r c) -> p r c", c=C)

            def normalise(src, n, mv_sem, ve_sem, rs_sem, cen_sem):
                pool.wait_ge(mv_sem, n + 1)
                nc.gpsimd.tensor_tensor(veps[:, :], var[:, :], eps_sb[:, :], ALU.add).then_inc(ve_sem, 1)
                nc.gpsimd.tensor_tensor(blocks(cen_g[:, :]), blocks(src[:, :]), by_row(mean[:, :]),
                                        ALU.subtract).then_inc(cen_sem, 1)
                pool.wait_ge(ve_sem, n + 1)
                nc.gpsimd.tensor_tensor(rstd[:, :], veps[:, :], mhalf[:, :], ALU.pow).then_inc(rs_sem, 1)
                pool.wait_ge(cen_sem, n + 1)
                pool.wait_ge(rs_sem, n + 1)

            def scaled(dst):
                return nc.gpsimd.tensor_tensor(blocks(dst), blocks(cen_g[:, :]), by_row(rstd[:, :]), ALU.mult)

            def ending(which, e, q):
                g = group(which, e)
                if which == 2:
                    if q == AT_NORM2:
                        normalise(h_g, e, mv2, ve2, rs2, cen2)
                    if q == AT_X1:
                        scaled(x1_g[:, :]).then_inc(x1_ready, 1)
                    if q == AT_X1_KEPT:
                        scaled(x_sb[:, g, :]).then_inc(x1_kept, 1)
                if which == 3:
                    n = e - NG
                    if q == AT_P_WHOLE:
                        if not isinstance(g, int):
                            pool.compute_val(p_hi[:, g, :].offset)
                        pool.wait_ge(p_ready, NG)
                        nc.gpsimd.tensor_tensor(p_g[:, :], p_hi[:, g, :].bitcast(f32), p_lo[:, g, :].bitcast(f32),
                                                ALU.add).then_inc(p_whole, 1)
                    if q == AT_Y:
                        if not isinstance(g, int):
                            pool.compute_val(x_sb[:, g, :].offset)
                        pool.wait_ge(x1_kept, NG)
                        pool.wait_ge(tanh_ready, n + 1)
                        nc.gpsimd.tensor_tensor(y_g[:, :], x_sb[:, g, :], th_g[:, :], ALU.add).then_inc(y_ready, 1)
                    if q == AT_NORM3:
                        normalise(y_g, n, mv3, ve3, rs3, cen3)
                    if q == AT_OUT:
                        if not (isinstance(n, int) and n == 0):
                            pool.wait_ge(stored, 16 * n)
                        scaled(o_g[:, :]).then_inc(out_ready, 1)

            def visit(which, e, before, par):
                for q in range(PAIRS):
                    cols = pool_cols(e, q)
                    if cols > 0:
                        pool.wait_ge(hi_ready, e * PAIRS + q + 1)
                        nc.gpsimd.tensor_tensor(lo[:, q % RING, :cols], vt[:, VEC.index(q) % 2, :cols],
                                                hi[:, q % RING, :cols].bitcast(f32), ALU.subtract)\
                            .then_inc(pool_lo_ready, 1)
                    if before:
                        ending(before, e - 1, q)

            for k in range(NK):
                q = 2 * k + 1
                pool.wait_ge(hi1_ready, PAIRS * LAST + (q + 1))
                nc.gpsimd.tensor_tensor(lo[:, q % RING, :], raw[:, k, 2:4, :].rearrange("p r n -> p (r n)"),
                                        hi[:, q % RING, :].bitcast(f32), ALU.subtract).then_inc(pool_lo1_ready, 1)

            run_visits(pool, visit)
            for q in range(PAIRS):
                ending(3, 2 * NG - 1, q)

        @block.scalar
        def _(act):
            act.dma_start(t_bc[:, :], t.rearrange("(a n) -> a n", a=1).to_broadcast([P, 1])).then_inc(t_in, 16)
            act.dma_start(ev[:, :].rearrange("p (k m) -> p k m", m=JB),
                          evals.rearrange("(k p m) -> p k m", p=P, m=JB)).then_inc(ev_in, 16)
            act.dma_start(w_sb[:, :], W).then_inc(w_in, 16)
            act.dma_start(b_bc[:, :], b.rearrange("(a n) -> a n", a=1).to_broadcast([P, C])).then_inc(b_in, 16)
            act.wait_ge(ev_in, 16)
            act.wait_ge(negt_ready, 1)
            nc.scalar.activation(coef[:, :], ev[:, :], ACT.Exp, scale=neg_t[:, 0:1]).then_inc(coef_ready, 1)

            def split_x(v, par):
                if isinstance(v, int) and v == 0:
                    act.wait_ge(x_in, 16)
                else:
                    act.wait_ge(x_rest_in, 16)
                nc.scalar.activation(xg_hi[:, par, :], x_sb[:, v, :], ACT.Copy).then_inc(xhi_ready, 1)

            def chunk1(v, k):
                act.wait_ge(raw_in[k], 16 * v + 16)
                for h in range(2):
                    q = 2 * k + h
                    if not (isinstance(v, int) and v == 0 and q < RING):
                        act.wait_ge(mm1_done, PAIRS * v + (q - RING + 1))
                    for r in (2 * h, 2 * h + 1):
                        last = nc.scalar.activation(hi[:, q % RING, (r % 2) * CW:(r % 2 + 1) * CW],
                                                    raw[:, k, r, :], ACT.Copy,
                                                    accum_out=rsum[:, v, r * NK + k:r * NK + k + 1])
                    last.then_inc(hi1_ready, 1)

            def visit1(v, par):
                for k in range(NK):
                    chunk1(v, k)
                    if k == NK // 2:
                        split_x(v + 1, 1 - par)

            split_x(0, 0)
            visit1(0, 0)
            with act.Fori(0, (NG - 2) // 2) as d:
                visit1(2 * d + 1, 1)
                visit1(2 * d + 2, 0)

            for i in range(NK + 4):
                if i < NK:
                    chunk1(LAST, i)
                if 0 <= (k := i - 4) < NK:
                    act.wait_ge(sT_done, k + 1)
                    if k == 0:
                        act.wait_ge(coef_ready, 1)
                    for jj in range(JB):
                        j = k * JB + jj
                        last = nc.scalar.activation(s_hi[:, j * C:(j + 1) * C], ps[:, k, jj * C:(jj + 1) * C],
                                                    ACT.Copy, scale=coef[:, j:j + 1])
                    last.then_inc(shi_ready, 1)

            def acc_to_stage(e, par):
                act.wait_ge(mm_done, (e + 1) * PAIRS)
                nc.scalar.activation(stage[:, 0, :], acc[:, par, :], ACT.Copy).then_inc(acc_out, 1)

            def ending(which, e, q, par):
                if q == AT_ACC:
                    acc_to_stage(e, par)
                if which == 2:
                    n, g = e, group(2, e)
                    if q == AT_X1T_OUT:
                        act.wait_ge(x1T_done, n + 1)
                        nc.scalar.activation(stage[:, 1, :], acc[:, par, :], ACT.Copy).then_inc(x1T_ready, 1)
                    if q == AT_P_OUT:
                        act.wait_ge(xw_done, n + 1)
                        nc.scalar.activation(p_hi[:, g, :], acc[:, par, :], ACT.Copy).then_inc(phi_ready, 1)
                if which == 3:
                    n, g = e - NG, group(3, e)
                    if q == AT_TANH:
                        act.wait_ge(pre3, n + 1)
                        nc.scalar.activation(th_g[:, :], h_g[:, :], ACT.Tanh).then_inc(tanh_ready, 1)
                    if q == AT_STORE:
                        act.wait_ge(out_ready, n + 1)
                        act.dma_start(out_v[g], o_g[:, :]).then_inc(stored, 16)

            def visit(which, e, before, par):
                for q in range(PAIRS):
                    if q in by_vector(e):
                        act.wait_ge(vturned, vturned_by(e, q))
                        src = vt[:, VEC.index(q) % 2, :]
                    else:
                        act.wait_ge(turned, turned_by(e, q))
                        slot = tslot(e, q)
                        src = ps[:, 2 * slot:2 * slot + 2, :]
                    if before or q >= RING:
                        act.wait_ge(mm_done, e * PAIRS + (q - RING + 1))
                    nc.scalar.activation(hi[:, q % RING, :], src, ACT.Copy)\
                        .then_inc(hi_ready, 1)
                    if before:
                        ending(before, e - 1, q, 1 - par)

            run_visits(act, visit)
            for q in range(PAIRS):
                ending(3, 2 * NG - 1, q, 1)
            act.wait_ge(stored, 16 * NG)

        @block.vector
        def _(dve):
            dve.wait_ge(t_in, 16)
            nc.vector.tensor_scalar(neg_t[:, :], t_bc[:, :], 1e-8, -1.0, ALU.max, ALU.mult).then_inc(negt_ready, 1)

            def split_x(v, par):
                dve.wait_ge(xhi_ready, v + 1)
                nc.vector.tensor_tensor(xg_lo[:, par, :], x_sb[:, v, :], xg_hi[:, par, :].bitcast(f32),
                                        ALU.subtract).then_inc(x_ready, 1)

            def half1(v, k, h):
                q = 2 * k + h
                dve.wait_ge(hi1_ready, PAIRS * v + (q + 1))
                nc.vector.tensor_tensor(lo[:, q % RING, :],
                                        raw[:, k, 2 * h:2 * h + 2, :].rearrange("p r n -> p (r n)"),
                                        hi[:, q % RING, :].bitcast(f32), ALU.subtract).then_inc(lo1_ready, 1)

            def chunk1(v, k):
                half1(v, k, 0)
                half1(v, k, 1)

            def visit1(v, par):
                for k in range(NK):
                    chunk1(v, k)
                    if k == NK // 2:
                        split_x(v + 1, 1 - par)

            split_x(0, 0)
            for k in range(NK):
                chunk1(0, k)
            split_x(1, 1)
            with dve.Fori(0, (NG - 2) // 2) as d:
                visit1(2 * d + 1, 1)
                visit1(2 * d + 2, 0)
            for i in range(NK + 4):
                if i < NK:
                    half1(LAST, i, 0)
                if 0 <= (k := i - 2) < NK:
                    dve.wait_ge(mm1_done, PAIRS * LAST + 2 * k + 2)
                    if k >= 2:
                        dve.wait_ge(sT_done, k - 1)
                    nc.vector.tensor_copy(stage[:, k % 2, :], ps[:, k, :]).then_inc(spec_out, 1)
                if 0 <= (k := i - 4) < NK:
                    dve.wait_ge(shi_ready, k + 1)
                    for jj in range(JB):
                        j = k * JB + jj
                        last = nc.vector.scalar_tensor_tensor(
                            out=s_lo[:, j * C:(j + 1) * C], in0=ps[:, k, jj * C:(jj + 1) * C],
                            scalar=coef[:, j:j + 1], in1=s_hi[:, j * C:(j + 1) * C].bitcast(f32),
                            op0=ALU.mult, op1=ALU.subtract)
                    last.then_inc(s_ready, 1)

            g_before = [None]

            def row_stats(src, ready, n, st):
                dve.wait_ge(ready, n + 1)
                for r in range(R):
                    last = nc.vector.bn_stats(stats[:, r, :], src[:, r * C:(r + 1) * C])
                last.then_inc(st, 1)

            def halves_of(n, st, halves):
                even, odd = stats[:, :, 0:3], stats[:, :, 3:6]
                dve.wait_ge(st, n + 1)
                nc.vector.tensor_tensor(msum[:, :], even[:, :, 1], odd[:, :, 1], ALU.add)
                nc.vector.tensor_tensor(mdif[:, :], even[:, :, 1], odd[:, :, 1], ALU.subtract)
                nc.vector.tensor_tensor(m2[:, :], even[:, :, 2], odd[:, :, 2], ALU.add).then_inc(halves, 1)

            def mean_of(n, halves, betw):
                dve.wait_ge(halves, n + 1)
                nc.vector.tensor_scalar(mean[:, :], msum[:, :], 0.5, None, ALU.mult)
                nc.vector.scalar_tensor_tensor(out=between[:, :], in0=mdif[:, :], scalar=0.25, in1=mdif[:, :],
                                               op0=ALU.mult, op1=ALU.mult).then_inc(betw, 1)

            def var_of(n, betw, done):
                dve.wait_ge(betw, n + 1)
                nc.vector.scalar_tensor_tensor(out=var[:, :], in0=m2[:, :], scalar=1.0 / C, in1=between[:, :],
                                               op0=ALU.mult, op1=ALU.add).then_inc(done, 1)

            def ending(which, e, q, par):
                g = g_before[0]
                if which == 2:
                    if q == AT_SUM:
                        dve.wait_ge(accT_done, e + 1)
                        nc.vector.tensor_tensor(h_g[:, :], acc[:, par, :], x_sb[:, g, :], ALU.add).then_inc(sum2, 1)
                    if q == AT_STATS2:
                        row_stats(h_g, sum2, e, st2)
                    if q == AT_HALVES2:
                        halves_of(e, st2, halves2)
                    if q == AT_MEAN2:
                        mean_of(e, halves2, betw2)
                    if q == AT_VAR2:
                        var_of(e, betw2, mv2)
                    if q == AT_P_OUT:
                        dve.wait_ge(phi_ready, e + 1)
                        nc.vector.tensor_tensor(p_lo[:, g, :], acc[:, par, :], p_hi[:, g, :].bitcast(f32),
                                                ALU.subtract).then_inc(p_ready, 1)
                if which == 3:
                    n = e - NG
                    if q == AT_SUM:
                        dve.wait_ge(accT_done, e + 1)
                        dve.wait_ge(p_whole, n + 1)
                        nc.vector.tensor_tensor(h_g[:, :], acc[:, par, :], p_g[:, :], ALU.add).then_inc(sum3, 1)
                    if q == AT_SCALE:
                        dve.wait_ge(sum3, n + 1)
                        for r in range(R):
                            last = nc.vector.scalar_tensor_tensor(
                                out=h_g[:, r * C:(r + 1) * C], in0=h_g[:, r * C:(r + 1) * C],
                                scalar=rdeg[:, g, r:r + 1], in1=b_bc[:, :], op0=ALU.mult, op1=ALU.add)
                        last.then_inc(pre3, 1)
                    if q == AT_STATS3:
                        row_stats(y_g, y_ready, n, st3)
                    if q == AT_HALVES3:
                        halves_of(n, st3, halves3)
                    if q == AT_MEAN3:
                        mean_of(n, halves3, betw3)
                    if q == AT_VAR3:
                        var_of(n, betw3, mv3)

            def visit(which, e, before, par):
                if before:
                    g_before[0] = group(before, e - 1)
                    if not isinstance(e, int):
                        dve.compute_val(x_sb[:, g_before[0], :].offset)
                for q in range(PAIRS):
                    cols = pool_cols(e, q)
                    if cols < 2 * CW:
                        if q in by_vector(e):
                            src = vt[:, VEC.index(q) % 2, :]
                        else:
                            slot = tslot(e, q)
                            src = ps[:, 2 * slot:2 * slot + 2, :].rearrange("p a n -> p (a n)")
                        dve.wait_ge(hi_ready, e * PAIRS + q + 1)
                        nc.vector.tensor_tensor(lo[:, q % RING, cols:], src[:, cols:],
                                                hi[:, q % RING, cols:].bitcast(f32), ALU.subtract)\
                            .then_inc(lo_ready, 1)
                    for v in by_vector(e):
                        if TURN_AT[v] == q:
                            turn(which, e, v)
                    if not before and q == AT_SUM:
                        degrees()
                    if before:
                        ending(before, e - 1, q, 1 - par)

            def degrees():
                nc.vector.tensor_reduce(rows[:, :, :], rsum[:, :, :].rearrange("p g (r k) -> p (g r) k", k=NK),
                                        mybir.AxisListType.X, ALU.add).then_inc(deg_s, 1)
                dve.wait_ge(deg_s, 1)
                nc.vector.tensor_scalar_add(deg[:, :, :], rows[:, :, :], 1.0).then_inc(deg_s, 1)
                dve.wait_ge(deg_s, 2)
                nc.vector.reciprocal(rdeg[:, :, :], deg[:, :, :]).then_inc(deg_s, 1)
                dve.wait_ge(deg_s, 3)

            def turn(which, e, q):
                n = VEC.index(q)
                k, half = PAIR_AT[q]
                dve.wait_ge(raw_in[k], arrived(which, e, k))
                if n >= 2:
                    wait_lo(dve, e, VEC[n - 2])
                elif not is_first(e - 1):
                    wait_lo(dve, e - 1, VEC[n - 2])
                m = 2 * half
                nc.vector.transpose(
                    vt[:, n % 2, :].rearrange("p (m b i) -> p m b i", m=2, b=RB),
                    raw[:, k].rearrange("p r w -> p (r w)").rearrange("p (b i m) -> p m b i", b=RB, m=JB)[:, m:m + 2])\
                    .then_inc(vturned, 1)

            dve.wait_ge(x_rest_in, 16)
            dve.wait_ge(b_in, 16)
            run_visits(dve, visit)
            g_before[0] = LAST
            for q in range(PAIRS):
                ending(3, 2 * NG - 1, q, 1)

        @block.tensor
        def _(pe):
            pe.wait_ge(ident_ready, 1)

            def chunk1(v, k, par, first, final):
                for h in range(2):
                    q = 2 * k + h
                    if not final:
                        pe.wait_ge(lo1_ready, PAIRS * v + (q + 1))
                    elif h == 0:
                        pe.wait_ge(lo1_ready, PAIRS * v + (k + 1))
                    else:
                        pe.wait_ge(pool_lo1_ready, k + 1)
                    for r in (2 * h, 2 * h + 1):
                        xh, xl = (a[:, par, r * C:(r + 1) * C] for a in (xg_hi, xg_lo))
                        ah, al = (a[:, q % RING, (r % 2) * CW:(r % 2 + 1) * CW] for a in (hi, lo))
                        nc.tensor.matmul(ps[:, k, :], xh, ah, start=first and r == 0, stop=False)
                        nc.tensor.matmul(ps[:, k, :], xh, al, start=False, stop=False)
                        last = nc.tensor.matmul(ps[:, k, :], xl, ah, start=False, stop=final and r == R - 1)
                    last.then_inc(mm1_done, 1)

            def visit1(v, par, first=False):
                pe.wait_ge(x_ready, v + 1)
                for k in range(NK):
                    chunk1(v, k, par, first, False)

            visit1(0, 0, first=True)
            with pe.Fori(0, (NG - 2) // 2) as d:
                visit1(2 * d + 1, 1)
                visit1(2 * d + 2, 0)
            pe.wait_ge(x_ready, NG)
            for i in range(NK + 2):
                if i < NK:
                    chunk1(LAST, i, 1, False, True)
                if 0 <= (k := i - 2) < NK:
                    pe.wait_ge(spec_out, k + 1)
                    for jj in range(JB):
                        last = nc.tensor.transpose(ps[:, k, jj * C:(jj + 1) * C],
                                                   spread(stage[:, k % 2, :], jj), ident[:, :])
                    last.then_inc(sT_done, 1)

            def turn(which, e, q):
                k, half = PAIR_AT[q]
                if half == 0:
                    pe.wait_ge(raw_in[k], arrived(which, e, k))
                for jj in range(2):
                    for r in range(R):
                        last = nc.tensor.transpose(ps[:, 2 * tslot(e, q) + jj, r * P:(r + 1) * P],
                                                   spread(raw[:, k, r, :], 2 * half + jj), ident[:, :])
                last.then_inc(turned, 1)

            def products(which, e, q, par):
                k, half = PAIR_AT[q]
                v_hi, v_lo = (s_hi, s_lo) if which == 2 else \
                    (a[:, :, :].rearrange("p g n -> p (g n)") for a in (p_hi, p_lo))
                out_t = acc[:, par, :]
                for jj in range(2):
                    j = k * JB + 2 * half + jj
                    vh, vl = (a[:, j * C:(j + 1) * C] for a in (v_hi, v_lo))
                    ah, al = (a[:, q % RING, jj * CW:(jj + 1) * CW] for a in (hi, lo))
                    nc.tensor.matmul(out_t, vh, ah, start=q == 0 and jj == 0, stop=False)
                    nc.tensor.matmul(out_t, vh, al, start=False, stop=False)
                    last = nc.tensor.matmul(out_t, vl, ah, start=False, stop=q == PAIRS - 1 and jj == 1)
                last.then_inc(mm_done, 1)

            def ending(which, e, q, par):
                bank = acc[:, par, :]
                if q == AT_TURN:
                    pe.wait_ge(acc_out, e + 1)
                    for r in range(R):
                        rows_r = stage[:, 0, r * P:(r + 1) * P] if isinstance(e, int) and e == 0 \
                            else spread(stage[:, 0, :], r)
                        last = nc.tensor.transpose(bank[:, r * C:(r + 1) * C], rows_r, ident[:, :])
                    last.then_inc(accT_done, 1)
                if which == 2 and q == AT_X1T:
                    pe.wait_ge(x1_ready, e + 1)
                    for r in range(R):
                        last = nc.tensor.transpose(bank[:, r * P:(r + 1) * P], x1_g[:, r * C:(r + 1) * C],
                                                   ident[:, :])
                    last.then_inc(x1T_done, 1)
                if which == 2 and q == AT_P:
                    pe.wait_ge(x1T_ready, e + 1)
                    for r in range(R):
                        last = nc.tensor.matmul(bank[:, r * C:(r + 1) * C], stage[:, 1, r * P:(r + 1) * P],
                                                w_sb[:, :], start=True, stop=True)
                    last.then_inc(xw_done, 1)

            def visit(which, e, before, par):
                for q in range(PAIRS):
                    if q >= LAG:
                        wait_lo(pe, e, q - LAG)
                    elif before:
                        wait_lo(pe, e - 1, PAIRS + q - LAG)
                    else:
                        pe.wait_ge(s_ready, 2 * tslot(e, q) + 2)
                    if q in by_tensor(e):
                        turn(which, e, q)
                    if q >= LAG:
                        if q == LAG:
                            if not before:
                                pe.wait_ge(s_ready, NK)
                            if which == 3 and before == 2:
                                pe.wait_ge(p_ready, NG - 1)
                        products(which, e, q - LAG, par)
                    elif before:
                        if before == 3 and PAIR_AT[PAIRS + q - LAG] == (0, 0):
                            pe.wait_ge(p_ready, NG)
                        products(before, e - 1, PAIRS + q - LAG, 1 - par)
                    if before:
                        ending(before, e - 1, q, 1 - par)

            pe.wait_ge(w_in, 16)
            run_visits(pe, visit)
            for q in range(PAIRS):
                if q < LAG:
                    wait_lo(pe, 2 * NG - 1, PAIRS + q - LAG)
                    products(3, 2 * NG - 1, PAIRS + q - LAG, 1)
                ending(3, 2 * NG - 1, q, 1)


_INS = ['x', 'adj', 'L0_gnn_evals', 'L0_gnn_t', 'L1_gnn_W', 'L1_gnn_b']


def kernel(**inputs):
    import numpy as _np
    import concourse.bacc as _bacc
    from concourse import mybir as _mybir
    from concourse.bass_utils import run_bass_kernel_spmd as _run

    nc = _bacc.Bacc("TRN2", target_bir_lowering=False, num_devices=1)
    arrays, args = {}, []
    for name in _INS:
        a = _np.ascontiguousarray(inputs[name])
        arrays[f"in_{name}_dram"] = a
        args.append(nc.dram_tensor(f"in_{name}_dram", a.shape, _mybir.dt.from_np(a.dtype), kind="ExternalInput").ap())
    shape = arrays["in_x_dram"].shape
    args.append(nc.dram_tensor("out_0_dram", shape, _mybir.dt.float32, kind="ExternalOutput").ap())
    spectral_then_graph_conv(nc, *args)
    r = _run(nc, [arrays], core_ids=[0])
    return r.results[0]["out_0_dram"]
```
